# Optimizing a Trainium2 kernel written in Bass

```python
import numpy as np
import jax
import jax.numpy as jnp

def _softmax(x, axis=-1):
    return jax.nn.softmax(x, axis=axis)

def _gelu(x):
    return jax.nn.gelu(x, approximate=True)

def _silu(x):
    return jax.nn.silu(x)

def _sigmoid(x):
    return jax.nn.sigmoid(x)

def _layernorm(x, axis=-1, eps=1e-05):
    m = jnp.mean(x, axis=axis, keepdims=True)
    v = jnp.var(x, axis=axis, keepdims=True)
    return (x - m) / jnp.sqrt(v + eps)

def _scatter_add(tgt, idx, src, axis=0):
    return tgt.at[idx].add(src)

def _segment_sum(src, seg, n):
    return jax.ops.segment_sum(src, seg, n)
kernel_name = 'mk_vit_tower_cls_d1_tok_img256_r4_8ce66e'

def setup_inputs(seed: int=0):
    np.random.seed(seed)
    _w = jnp.asarray

    def _rec_inputs():
        import jax
        import jax.numpy as jnp
        _rk = jax.random.key(seed)
        x = -0.000596345 + 1.00056 * jax.random.normal(jax.random.fold_in(_rk, 1), (64, 64, 64, 3), jnp.float32)
        cls_tok = 0.02 * jax.random.normal(jax.random.fold_in(_rk, 5), (1, 1, 64), jnp.float32)
        return (x, cls_tok)
    x, cls_tok = _rec_inputs()

    def _L0_tok_setup():
        import jax, jax.numpy as jnp
        import numpy as np
        M1, M2, WIDTH, LAYERS = (16, 16, 64, 4)
        B, H, W = (16, 64, 64)
        EPS = 1e-05

        def _spectral_conv(h, w1, w2):
            xf = jnp.fft.rfft2(h)
            top = jnp.einsum('bixy,ioxy->boxy', xf[:, :, :M1, :M2], w1)
            bot = jnp.einsum('bixy,ioxy->boxy', xf[:, :, -M1:, :M2], w2)
            of = jnp.zeros(xf.shape, dtype=xf.dtype)
            of = of.at[:, :, :M1, :M2].set(top)
            of = of.at[:, :, -M1:, :M2].set(bot)
            return jnp.fft.irfft2(of, s=(h.shape[-2], h.shape[-1]))
        key = jax.random.key(seed)
        ks = jax.random.split(key, 16)
        scale = 1.0 / (WIDTH * WIDTH)
        inp = {'x': jax.random.normal(ks[0], (B, H, W, 3), dtype=jnp.float32), 'fc0_w': jax.random.normal(ks[1], (3, WIDTH), dtype=jnp.float32) * 0.3, 'fc0_b': jnp.zeros((WIDTH,), jnp.float32), 'w1r': jax.random.normal(ks[2], (LAYERS, WIDTH, WIDTH, M1, M2), dtype=jnp.float32) * scale, 'w1i': jax.random.normal(ks[3], (LAYERS, WIDTH, WIDTH, M1, M2), dtype=jnp.float32) * scale, 'w2r': jax.random.normal(ks[4], (LAYERS, WIDTH, WIDTH, M1, M2), dtype=jnp.float32) * scale, 'w2i': jax.random.normal(ks[5], (LAYERS, WIDTH, WIDTH, M1, M2), dtype=jnp.float32) * scale, 'pw_w': jax.random.normal(ks[6], (LAYERS, WIDTH, WIDTH), dtype=jnp.float32) * (1.0 / np.sqrt(WIDTH)), 'pw_b': jnp.zeros((LAYERS, WIDTH), jnp.float32), 'gamma': jnp.ones((LAYERS, WIDTH), jnp.float32), 'beta': jnp.zeros((LAYERS, WIDTH), jnp.float32), 'fc1_w': jax.random.normal(ks[7], (WIDTH, 128), dtype=jnp.float32) * (1.0 / np.sqrt(WIDTH)), 'fc1_b': jnp.zeros((128,), jnp.float32), 'fc2_w': jax.random.normal(ks[8], (128, 1), dtype=jnp.float32) * (1.0 / np.sqrt(128.0)), 'fc2_b': jnp.zeros((1,), jnp.float32)}
        return inp
    _L0_tok_all = _L0_tok_setup()
    _L0_tok_in = {k: v for k, v in _L0_tok_all.items() if k in ('fc0_w', 'fc0_b', 'w1r', 'w1i', 'w2r', 'w2i', 'pw_w', 'pw_b', 'gamma', 'beta', 'fc1_w', 'fc1_b', 'fc2_w', 'fc2_b')}
    del _L0_tok_all

    def _L0_attn_setup():
        import jax, jax.numpy as jnp
        import numpy as np
        B, S, C = (8, 256, 64)
        H, KD = (8, 64)
        HEAD_DIM = KD // H
        key = jax.random.key(seed)
        ks = jax.random.split(key, 5)
        sc = 0.02
        return {'x': jax.random.normal(ks[0], (B, S, C), dtype=jnp.float32), 'Wq': jax.random.normal(ks[1], (H * KD, C), dtype=jnp.float32) * sc, 'Wk': jax.random.normal(ks[2], (KD, C), dtype=jnp.float32) * sc, 'Wv': jax.random.normal(ks[3], (KD, C), dtype=jnp.float32) * sc, 'Wo': jax.random.normal(ks[4], (C, H * KD), dtype=jnp.float32) * sc}
    _L0_attn_all = _L0_attn_setup()
    _L0_attn_in = {k: v for k, v in _L0_attn_all.items() if k in ('Wq', 'Wk', 'Wv', 'Wo')}
    del _L0_attn_all

    def _L0_ffn_setup():
        import jax, jax.numpy as jnp
        import numpy as np
        C = 64
        HID = 256
        E = 8
        TEMP = 1.0
        key = jax.random.key(seed)
        ks = jax.random.split(key, 7)
        x = jax.random.normal(ks[0], (8, 4096, C), dtype=jnp.float32)
        W1 = jax.random.normal(ks[1], (C, HID), dtype=jnp.float32) * 0.02
        b1 = jnp.zeros((HID,), dtype=jnp.float32)
        Wg = jax.random.normal(ks[2], (HID, E), dtype=jnp.float32) * 0.02
        bg = jnp.zeros((E,), dtype=jnp.float32)
        Wd = jax.random.normal(ks[3], (E, HID, C), dtype=jnp.float32) * 0.02
        bd = jnp.zeros((E, C), dtype=jnp.float32)
        return {'x': x, 'W1': W1, 'b1': b1, 'Wg': Wg, 'bg': bg, 'Wd': Wd, 'bd': bd}
    _L0_ffn_all = _L0_ffn_setup()
    _L0_ffn_in = {k: v for k, v in _L0_ffn_all.items() if k in ('W1', 'b1', 'Wg', 'bg', 'Wd', 'bd')}
    del _L0_ffn_all
    return {'x': x, 'cls_tok': cls_tok, 'L0_tok_fc0_w': _L0_tok_in['fc0_w'], 'L0_tok_fc0_b': _L0_tok_in['fc0_b'], 'L0_tok_w1r': _L0_tok_in['w1r'], 'L0_tok_w1i': _L0_tok_in['w1i'], 'L0_tok_w2r': _L0_tok_in['w2r'], 'L0_tok_w2i': _L0_tok_in['w2i'], 'L0_tok_pw_w': _L0_tok_in['pw_w'], 'L0_tok_pw_b': _L0_tok_in['pw_b'], 'L0_tok_gamma': _L0_tok_in['gamma'], 'L0_tok_beta': _L0_tok_in['beta'], 'L0_tok_fc1_w': _L0_tok_in['fc1_w'], 'L0_tok_fc1_b': _L0_tok_in['fc1_b'], 'L0_tok_fc2_w': _L0_tok_in['fc2_w'], 'L0_tok_fc2_b': _L0_tok_in['fc2_b'], 'L0_attn_Wq': _L0_attn_in['Wq'], 'L0_attn_Wk': _L0_attn_in['Wk'], 'L0_attn_Wv': _L0_attn_in['Wv'], 'L0_attn_Wo': _L0_attn_in['Wo'], 'L0_ffn_W1': _L0_ffn_in['W1'], 'L0_ffn_b1': _L0_ffn_in['b1'], 'L0_ffn_Wg': _L0_ffn_in['Wg'], 'L0_ffn_bg': _L0_ffn_in['bg'], 'L0_ffn_Wd': _L0_ffn_in['Wd'], 'L0_ffn_bd': _L0_ffn_in['bd']}

def reference(x, cls_tok, L0_tok_fc0_w, L0_tok_fc0_b, L0_tok_w1r, L0_tok_w1i, L0_tok_w2r, L0_tok_w2i, L0_tok_pw_w, L0_tok_pw_b, L0_tok_gamma, L0_tok_beta, L0_tok_fc1_w, L0_tok_fc1_b, L0_tok_fc2_w, L0_tok_fc2_b, L0_attn_Wq, L0_attn_Wk, L0_attn_Wv, L0_attn_Wo, L0_ffn_W1, L0_ffn_b1, L0_ffn_Wg, L0_ffn_bg, L0_ffn_Wd, L0_ffn_bd):
    import jax
    import jax.numpy as jnp

    def _L0_tok_ref(x, fc0_w, fc0_b, w1r, w1i, w2r, w2i, pw_w, pw_b, gamma, beta, fc1_w, fc1_b, fc2_w, fc2_b):
        import jax, jax.numpy as jnp
        import numpy as np
        M1, M2, WIDTH, LAYERS = (16, 16, 64, 4)
        B, H, W = (16, 64, 64)
        EPS = 1e-05

        def _spectral_conv(h, w1, w2):
            xf = jnp.fft.rfft2(h)
            top = jnp.einsum('bixy,ioxy->boxy', xf[:, :, :M1, :M2], w1)
            bot = jnp.einsum('bixy,ioxy->boxy', xf[:, :, -M1:, :M2], w2)
            of = jnp.zeros(xf.shape, dtype=xf.dtype)
            of = of.at[:, :, :M1, :M2].set(top)
            of = of.at[:, :, -M1:, :M2].set(bot)
            return jnp.fft.irfft2(of, s=(h.shape[-2], h.shape[-1]))
        h = jnp.einsum('bhwi,ic->bhwc', x, fc0_w) + fc0_b
        h = h.transpose(0, 3, 1, 2)
        for l in range(LAYERS):
            sc = _spectral_conv(h, w1r[l] + 1j * w1i[l], w2r[l] + 1j * w2i[l])
            pw = jnp.einsum('bihw,oi->bohw', h, pw_w[l]) + pw_b[l][None, :, None, None]
            y = sc + pw
            mean = y.mean(axis=(0, 2, 3), keepdims=True)
            var = y.var(axis=(0, 2, 3), keepdims=True)
            y = (y - mean) * jax.lax.rsqrt(var + EPS)
            y = y * gamma[l][None, :, None, None] + beta[l][None, :, None, None]
            h = jax.nn.gelu(y, approximate=False)
        h = h.transpose(0, 2, 3, 1)
        h = jax.nn.gelu(h @ fc1_w + fc1_b, approximate=False)
        out = (h @ fc2_w + fc2_b).squeeze(-1)
        return out

    def _L0_attn_ref(x, Wq, Wk, Wv, Wo):
        import jax, jax.numpy as jnp
        import numpy as np
        B, S, C = (8, 256, 64)
        H, KD = (8, 64)
        HEAD_DIM = KD // H
        b, s, c = x.shape
        q = jnp.einsum('bsc,oc->bso', x, Wq).reshape(b, s, H, KD).transpose(0, 2, 1, 3)
        k = jnp.einsum('bsc,oc->bos', x, Wk)
        v_conv = jnp.einsum('bsc,oc->bos', x, Wv)
        v = v_conv.reshape(b, s, KD)
        scale = 1.0 / np.sqrt(HEAD_DIM).astype(np.float32)
        scores = jnp.einsum('bhsd,bdt->bhst', q, k) * scale
        attn = jax.nn.softmax(scores, axis=-1)
        ctx = jnp.einsum('bhst,btd->bhsd', attn, v)
        ctx = ctx.transpose(0, 2, 1, 3).reshape(b, H * KD, s)
        out = jnp.einsum('bcp,oc->bop', ctx, Wo)
        return out.transpose(0, 2, 1)

    def _L0_ffn_ref(x, W1, b1, Wg, bg, Wd, bd):
        import jax, jax.numpy as jnp
        import numpy as np
        C = 64
        HID = 256
        E = 8
        TEMP = 1.0
        orig_shape = x.shape
        xf = x.reshape(-1, orig_shape[-1])
        H = jax.nn.gelu(xf @ W1 + b1, approximate=False)
        probs = jax.nn.softmax((H @ Wg + bg) / TEMP, axis=-1)
        assign = jnp.argmax(probs, axis=-1)
        out = jnp.zeros_like(xf)
        for e in range(Wd.shape[0]):
            y = H @ Wd[e] + bd[e]
            sel = (assign == e)[:, None]
            out = out + jnp.where(sel, probs[:, e:e + 1] * y, 0.0)
        return out.reshape(orig_shape)
    h = _L0_tok_ref(x, L0_tok_fc0_w, L0_tok_fc0_b, L0_tok_w1r, L0_tok_w1i, L0_tok_w2r, L0_tok_w2i, L0_tok_pw_w, L0_tok_pw_b, L0_tok_gamma, L0_tok_beta, L0_tok_fc1_w, L0_tok_fc1_b, L0_tok_fc2_w, L0_tok_fc2_b)
    h = jnp.concatenate([jnp.broadcast_to(cls_tok, (h.shape[0], 1, h.shape[2])), h], axis=1)
    h = h + _L0_attn_ref(_layernorm(h, axis=-1), L0_attn_Wq, L0_attn_Wk, L0_attn_Wv, L0_attn_Wo)
    h = h + _L0_ffn_ref(_layernorm(h, axis=-1), L0_ffn_W1, L0_ffn_b1, L0_ffn_Wg, L0_ffn_bg, L0_ffn_Wd, L0_ffn_bd)
    return h

_drawn_inputs = setup_inputs


def setup_inputs(seed=0):
    import zlib

    import numpy as np

    out = dict(_drawn_inputs(seed))
    spreads = {'L0_tok_fc0_b': (0.0, 0.8),
     'L0_tok_pw_b': (0.0, 0.8),
     'L0_tok_gamma': (1.0, 0.2),
     'L0_tok_beta': (0.0, 0.1),
     'L0_tok_fc1_b': (0.0, 0.1),
     'L0_ffn_b1': (0.0, 0.8),
     'L0_ffn_bg': (0.0, 0.1),
     'L0_ffn_bd': (0.0, 0.297)}
    factors = {'cls_tok': 8.0,
     'L0_tok_w1r': 8.0,
     'L0_tok_w1i': 8.0,
     'L0_tok_w2r': 8.0,
     'L0_tok_w2i': 8.0,
     'L0_attn_Wq': 8.0,
     'L0_attn_Wk': 8.0,
     'L0_attn_Wv': 3.047,
     'L0_attn_Wo': 3.101,
     'L0_ffn_W1': 6.036,
     'L0_ffn_Wg': 8.0,
     'L0_ffn_Wd': 6.221}
    for name, (base, spread) in spreads.items():
        noise = np.random.default_rng([zlib.crc32(name.encode()), seed]).standard_normal(out[name].shape)
        drawn = base * np.exp(spread * noise) if base else spread * noise
        out[name] = jnp.asarray(drawn.astype(out[name].dtype))
    for name, factor in factors.items():
        out[name] = (out[name] * factor).astype(out[name].dtype)
    return out
```

```python
from contextlib import ExitStack

import numpy as np

import concourse.bass as bass
from concourse import mybir

F32 = mybir.dt.float32
F32R = mybir.dt.float32r
BF16 = mybir.dt.bfloat16
ALU = mybir.AluOpType
ACT = mybir.ActivationFunctionType
AX = mybir.AxisListType

P = 128
B, C, S = 64, 64, 64
PIX = S * S
PAIRS = B // 2
KX, KY = 32, 16
LAYERS = 4
CH = 8
KC = KX // CH
MODES = KC * KY
EPS = 1e-5
T = S + 1
HEADS = 8
TT, TILES = 104, 20
HALF = TT * TILES
G_XT, G_K, G_V, G_Q, G_WO, G_XT2, G_H, G_LG, G_Y = (
    int(n) for n in np.cumsum([0, 3, 4, 4, 32, 3, 3, 10, 1]))
HID = 128
SLOT = 1024
LEAD = 1
NORM = B * PIX

INV = ["mT", "ih0", "ih1", "gT0", "gT1", "iw0", "iw1", "iw2", "iw3"]
FWD = ["pw0", "pw1", "pw2", "pw3", "hT0", "hT1", "hT2", "hT3", "fw0", "fw1", "fw2", "fw3",
       "dT0", "dT1", "fh0", "fh1"]
OUT = [f"fc{k}" for k in range(8)] + ["sum"]
ORDER = {
    "first": ["pw0", "hT0", "pw1", "hT1", "pw2", "hT2", "pw3", "hT3", "fw0", "iw0", "fw1", "iw1", "fw2",
              "iw2", "fw3", "iw3", "dT0", "dT1", "fh0", "fh1"],
    "middle": ["pw0", "mT", "hT0", "pw1", "ih0", "hT1", "pw2", "ih1", "hT2", "pw3", "gT0", "hT3", "fw0",
               "gT1", "fw1", "iw0", "fw2", "iw1", "fw3", "iw2", "dT0", "iw3", "dT1", "fh0", "fh1"],
    "last": ["fc0", "mT", "fc1", "ih0", "fc2", "ih1", "fc3", "gT0", "fc4", "gT1", "fc5", "iw0", "fc6",
             "iw1", "fc7", "iw2", "iw3", "sum"],
}


def slot_table(order):
    table = {step: n % 4 for n, step in enumerate(order)}
    if len(order) % 4 == 1:
        table[order[-1]] = 1
    return table


SLOTS = {kind: slot_table(order) for kind, order in ORDER.items()}


def quarter(step):
    return int(step[2]) if step[2:3].isdigit() else 0


def is_inverse(step):
    return step in INV


def steps_of(kind, part):
    return [s for s in ORDER[kind]
            if part == "body" or (part == "head") == is_inverse(s)]


def uses(kind, steps, slot):
    return sum(SLOTS[kind][s] == slot for s in steps)


def pass_uses(kind):
    return [PAIRS * uses(kind, ORDER[kind], s) for s in range(4)]


MIX_USES = [2 * CH] * 3 + [2 * CH + 1]
FIRST_USES, MIDDLE_USES, LAST_USES = (pass_uses(k) for k in ("first", "middle", "last"))


def fills(kind, part, j, step, base):
    slot = SLOTS[kind][step]
    steps = steps_of(kind, part)
    n = uses(kind, steps[:steps.index(step) + 1], slot)
    if part == "head":
        return base[slot] + n
    per = uses(kind, ORDER[kind], slot)
    forward = uses(kind, steps_of(kind, "tail"), slot)
    return base[slot] + j * per + (n - forward)


def once_before(kind, j, step, base):
    slot = SLOTS[kind][step]
    order = ORDER[kind]
    n = uses(kind, order[:order.index(step) + 1], slot) - uses(kind, steps_of(kind, "tail"), slot)
    return base[slot] + (j - 1) * uses(kind, order, slot) + n




def dft_constants():
    w = np.arange(S)
    ky, kx = np.arange(KY), np.concatenate([np.arange(KX // 2), np.arange(S - KX // 2, S)])
    kw = 2 * np.pi * np.outer(ky, w) / S
    kh = 2 * np.pi * np.outer(kx, w) / S
    fw = np.zeros((2, S, P))
    for h2 in range(2):
        v = fw[h2, :, :64].reshape(S, KY, 2, 2)
        v[:, :, h2, 0] = np.cos(kw).T
        v[:, :, h2, 1] = -np.sin(kw).T
    fh = np.zeros((S, 2, 4, KX))
    fh[:, 0, 0], fh[:, 1, 0] = np.cos(kh).T, np.sin(kh).T
    fh[:, 0, 1], fh[:, 1, 1] = -np.sin(kh).T, np.cos(kh).T
    fh[:, :, 2] = -fh[:, :, 1]
    eh = np.zeros((KX, 2, 2, S, 2, 2))
    for x in range(KX):
        for y in range(2):
            eh[x, 0, y, :, y, 0], eh[x, 1, y, :, y, 0] = np.cos(kh[x]), -np.sin(kh[x])
            eh[x, 0, y, :, y, 1], eh[x, 1, y, :, y, 1] = np.sin(kh[x]), np.cos(kh[x])
    ew = np.zeros((4, KY, 2, 4, S))
    order = ky.reshape(2, KY // 2).T.reshape(-1)
    ck = (np.where(ky == 0, 1.0, 2.0)[:, None] / PIX)[order]
    for h4 in range(4):
        ew[h4, :, 0, h4], ew[h4, :, 1, h4] = ck * np.cos(kw[order]), -ck * np.sin(kw[order])
    dup = (np.arange(P)[:, None] % C == np.arange(P)[None, :] % C)
    sq = np.array([1, 2 / PIX, .5 / PIX, 2 / PIX, 1 / PIX, 1 / PIX, -1 / PIX, .5 / PIX, -.5 / PIX, 0, 0, 0]) / NORM
    av = np.array([0] * 9 + [1, .5, 0]) / NORM
    parts = [("ident", np.eye(P)), ("fw", fw.reshape(P, -1)), ("fh", fh.reshape(P, -1)),
             ("eh", eh.reshape(P, -1)), ("ew", ew.reshape(P, -1)), ("dup", dup),
             ("sq", np.tile(sq, (P, 1))), ("av", np.tile(av, (P, 1))),
             ("first", np.tile(8.0 - np.arange(8), (P, 1)))]
    where, at = {}, 0
    for name, m in parts:
        where[name] = (at, m.shape[1])
        at += m.shape[1]
    return np.concatenate([m for _, m in parts], axis=1).astype(np.float32), where


def build(nc, x_p, cls_tok, fc0_w, fc0_b, w_modes, pw_t, chan, fc1_w, fc1_b, fc2_w, fc2_b,
          wq_t, wk_t, wv_t, wo_t, w1, b1, wg, bg, wd, bd, consts, out, where):
    ctx = ExitStack()
    with ctx:
        def sb(name, shape, dt=F32):
            return ctx.enter_context(nc.sbuf_tensor(name, shape, dt))

        def sem(name):
            return ctx.enter_context(nc.semaphore(name))

        con = sb("con", [P, consts.shape[1]])

        def const(name):
            at, n = where[name]
            return con[:, at:at + n]

        ident, fw_m, fh_m, dup = (const(n) for n in ("ident", "fw", "fh", "dup"))
        inv_s = sb("inv_s", [P, 2, 512], F32R)
        inv_m = con[:, where["eh"][0]:where["eh"][0] + 512]
        eh_m, ew_m = ([inv_s[:, i, n * 256:(n + 1) * 256] for i in range(2)] for n in range(2))
        pwt = sb("pwt", [P, P])
        fc0 = sb("fc0", [P, P])
        fc1 = sb("fc1", [P, 2, HID])
        pws = sb("pws", [P, 2, P], F32R)
        fc1s = sb("fc1s", [P, 2, 2, HID], F32R)
        fc2 = sb("fc2", [P, 80], F32R)
        fc2c = sb("fc2c", [P, 1])
        vec = sb("vec", [P, 3])
        chn = sb("chn", [P, LAYERS, 3])
        cur = sb("cur", [P, 3])
        zacc = sb("zacc", [P, 4])
        zsum = sb("zsum", [P, 4])
        eacc = sb("eacc", [P, 2, KY])
        esum = sb("esum", [P, 2, KY])
        zdc = sb("zdc", [P, 4])
        st = sb("st", [P, 12])
        tmp = sb("tmp", [P, 2, 12])
        mom = sb("mom", [P, 12])
        with ExitStack() as region:
            def place(name, n, dt=F32, parts=P):
                return region.enter_context(nc.sbuf_tensor(name, [parts, n], dt))[:, :]

            def place_parts(name, n):
                return place(name, 2 * n, F32R).rearrange("p (s c) -> p s c", s=2)

            zy = place("zy", PIX)
            hh = place("hh", PIX)
            hs = place_parts("hs", PIX)
            ms = place("ms", 2 * KX * KY)
            mt = place_parts("mt", 8 * P)
            gg = place("gg", KY * P)
            gt = place_parts("gt", KY * P)
            outer = region
            with ExitStack() as region:
                zo = place("zo", PIX)
                ht = place("ht", PIX)
                d1 = place("d1", KY * P)
                d1t = place("d1t", KY * P)
                d2 = place("d2", 3 * KX * KY)
                y0 = place("y0", PIX)
                junk = place("junk", 4096, BF16)
            with ExitStack() as region:
                gf = [place(f"gf{i}", SLOT) for i in range(2)]
                g_hi = [place(f"g_hi{i}", SLOT, F32R) for i in range(8)]
                g_lo = [place(f"g_lo{i}", SLOT, F32R) for i in range(8)]
                ot = place("ot", 512, parts=16)
                ot_lo = place("ot_lo", 512, parts=16)
            region = outer
        with ExitStack() as region:
            wb = [place(f"wb{i}", 8192) for i in range(2)]
            xb = [place(f"xb{i}", 8192) for i in range(2)]
            mo = place("mo", 8192)
            mjunk = place("mjunk", 4096, BF16)
            m0 = place("m0", KX * 2 * B, parts=C)
            xp = wb[0][0:C, 0:15 * 2 * B]

        ps = [ctx.enter_context(nc.psum_tensor(f"ps{i}", [P, SLOT], F32)) for i in range(4)]

        zd = nc.dram_tensor("z_d", [PAIRS, P, PIX], F32).ap()
        ad = nc.dram_tensor("a_d", [CH, 3, C, B, MODES], F32).ap()
        md = nc.dram_tensor("m_d", [CH, C, B, 2 * MODES], F32).ap()
        tok = nc.dram_tensor("tok_d", [B, S + 1, S], F32).ap()

        filled = [sem(f"filled{i}") for i in range(4)]
        freed = [sem(f"freed{i}") for i in range(4)]
        consts_in = sem("consts_in")
        zeroed = sem("zeroed")
        small_in = sem("small_in")
        fc2_ready = sem("fc2_ready")
        x_in = sem("x_in")
        z_in = [sem(f"z_in{k}") for k in range(4)]
        m_in = sem("m_in")
        pw_in = sem("pw_in")
        h_ready = [sem(f"h_ready{k}") for k in range(4)]
        z_out = [sem(f"z_out{k}") for k in range(4)]
        a_out = sem("a_out")
        t_out = sem("t_out")
        squared = sem("squared")
        z_summed = sem("z_summed")
        arena_free = sem("arena_free")
        pw_split = sem("pw_split")
        fc_split = sem("fc_split")
        hi_taken = sem("hi_taken")
        h_hi = sem("h_hi")
        h_split = [sem(f"h_split{k}") for k in range(4)]
        g_rounded = sem("g_rounded")
        g_split = [sem(f"g_split{i}") for i in range(2)]
        ot_ready = sem("ot_ready")
        pw_spread = sem("pw_spread")
        wx_in = [sem(f"wx_in{i}") for i in range(2)]
        m_out = [sem(f"m_out{i}") for i in range(2)]
        m_taken = sem("m_taken")
        e_summed = sem("e_summed")
        stats = sem("stats")
        stats_chain = sem("stats_chain")
        root = sem("root")
        norm_ready = sem("norm_ready")
        cls_out = sem("cls_out")
        scale_v, shift_v = mom[:, 8:9], mom[:, 9:10]
        N_STATS = 42

        def rounds():
            def mix_base(l):
                return [LEAD + FIRST_USES[s] + l * (MIX_USES[s] + MIDDLE_USES[s]) for s in range(4)]
            return mix_base

        mix_base = rounds()

        def pass_base(l):
            return [b + m for b, m in zip(mix_base(l), MIX_USES)]

        arena = sb("arena", [P, 43008])
        at = 0

        def take(n, parts=P):
            nonlocal at
            at += n
            return arena[0:parts, at - n:at]

        tokm = take(TILES * 2 * S, TT)
        xn = take(TILES * 2 * S, TT)
        xt = take(HALF)
        qt = take(HALF * HEADS)
        ct = qt
        yb = [qt[0:TT, i * 1024:(i + 1) * 1024] for i in range(2)]
        kb = take(B // 2 * 2 * T)
        vc = take(HALF)
        vv = take(B * S, T)
        k_at = at - B * S - HALF - B * T
        hid = arena[:, k_at:k_at + 4 * HALF]
        wq_m, wk_m, wv_m = take(HEADS * P), take(P), take(P)
        wo_m = take(4 * S)
        w1_m = take(2 * 2 * P)
        wg_m = take(2 * 8)
        wd_m = take(2 * 8 * C)
        bd_m = take(8 * C, TT)
        bg_m = take(8, TT)
        b1_m = take(2)
        ss = take(10 * T, TT)
        ex = take(10 * T, TT)
        qb = take(520)
        attn_t = take(1040, T)
        co = take(640, TT)
        lnw = qt[0:TT, 8192:8192 + 2560]
        red = take(40, TT)
        mean_t, var_t, rt_t, inv_t, nw_t = (take(40, TT) for _ in range(5))
        mx, sm, rc = (take(10, TT) for _ in range(3))
        lg, eq, gate = (take(320, TT) for _ in range(3))
        assert at <= 43008, at
        vd = nc.dram_tensor("v_d", [B, S * T], F32).ap()
        cd = nc.dram_tensor("c_d", [B, HEADS * T * S], F32).ap()

        weights_in = sem("weights_in")
        blank = sem("blank")
        tok_in = sem("tok_in")
        ln_root = sem("ln_root")
        link_t = sem("link_t")
        xn_ready = sem("xn_ready")
        v_out = sem("v_out")
        v_in = sem("v_in")
        qb_ready = sem("qb_ready")
        s_full, s_read = sem("s_full"), sem("s_read")
        e_ready = sem("e_ready")
        t_full, t_read = sem("t_full"), sem("t_read")
        c_full, c_read = sem("c_full"), sem("c_read")
        c_out = sem("c_out")
        c_in = sem("c_in")
        g_exp = sem("g_exp")
        res_ready = sem("res_ready")
        res_out = sem("res_out")
        tail = [b + n for b, n in zip(pass_base(LAYERS - 1), LAST_USES)]

        def gfill(g):
            return tail[g % 4] + g // 4 + 1

        block = ctx.enter_context(nc.Block())

        @block.sync
        def _(sp):
            for s in (*filled, *freed, *z_out, *m_out, *g_split, squared, z_summed, a_out, e_summed, t_out,
                      c_full, t_read, c_read, c_out, s_full):
                sp.sem_inc(s, LEAD)
            sp.dma_start(con[:, :], consts).then_inc(consts_in, 16)
            sp.wait_ge(zeroed, 1)
            for i in range(2):
                r = slice(i * C, (i + 1) * C)
                sp.dma_start(fc0[3 * i:3 * i + 3, r], fc0_w).then_inc(small_in, 16)
                sp.dma_start(fc1[r, i, :], fc1_w).then_inc(small_in, 16)
                sp.dma_start(vec[r, 0:1], fc0_b).then_inc(small_in, 16)
                sp.dma_start(chn[r, :, :], chan).then_inc(small_in, 16)
            sp.dma_start(vec[:, 1:2], fc1_b).then_inc(small_in, 16)
            sp.dma_start(vec[:, 2:3], fc2_b.to_broadcast([P, 1])).then_inc(small_in, 16)
            sp.dma_start(fc2c[:, :], fc2_w).then_inc(small_in, 16)

            def load_pw(layer):
                for i in range(2):
                    r = slice(i * C, (i + 1) * C)
                    sp.dma_start(pwt[r, r], pw_t[layer]).then_inc(pw_in, 16)

            def load_pair(kind, q, j):
                if kind == "first":
                    sp.dma_start(zy[0:6, :], x_p[j]).then_inc(x_in, 16)
                    return
                for i in range(2):
                    src = md[:, :, 2 * j + i, :].rearrange("c o m -> o c m")
                    dst = ms[i * C:(i + 1) * C, :].rearrange("p (c m) -> p c m", c=CH)
                    sp.dma_start(dst, src).then_inc(m_in, 16)

            def run_pass(kind, q, base):
                def iteration(part, j, more=True):
                    order = steps_of(kind, part)
                    for step in order:
                        done = (kind, part, j, step, base)
                        slot = SLOTS[kind][step]
                        if step.startswith("pw"):
                            k = int(step[2])
                            sp.wait_ge(freed[slot], fills(*done))
                            sp.dma_start(zd[j - 1, :, k * SLOT:(k + 1) * SLOT],
                                         zo[:, k * SLOT:(k + 1) * SLOT]).then_inc(z_out[k], 16)
                        if step == "mT" and more:
                            sp.wait_ge(filled[slot], fills(*done))
                            load_pair(kind, q, j + 1)
                        if step.startswith("iw") and more:
                            k = int(step[2])
                            if kind == "first":
                                if k == 3:
                                    sp.wait_ge(filled[slot], fills(*done))
                                    load_pair(kind, q, j + 1)
                            else:
                                sp.wait_ge(h_ready[k], q * PAIRS + j + 1)
                                sp.dma_start(zy[:, k * SLOT:(k + 1) * SLOT],
                                             zd[j + 1, :, k * SLOT:(k + 1) * SLOT]).then_inc(z_in[k], 16)
                        if step == "fh1":
                            sp.wait_ge(freed[slot], fills(*done))
                            for i in range(2):
                                for b in range(3):
                                    src = d2[i * C:(i + 1) * C, b * 512:(b + 1) * 512]
                                    dst = ad[:, b, :, 2 * (j - 1) + i, :].rearrange("k c m -> c k m")
                                    sp.dma_start(dst, src.rearrange("p (k m) -> p k m", k=CH))\
                                        .then_inc(a_out, 16)
                        if step == "sum":
                            sp.wait_ge(freed[slot], fills(*done))
                            dst = tok[bass.ds(2 * (j - 1), 2), 1:S + 1, :] if not isinstance(j, int) else \
                                tok[2 * (j - 1):2 * j, 1:S + 1, :]
                            for i in range(2):
                                sp.dma_start(dst[i].rearrange("(t r) w -> t (r w)", t=8),
                                             ot[8 * i:8 * i + 8, :]).then_inc(t_out, 16)

                load_pair(kind, q, 0)
                if kind != "first":
                    for k in range(4):
                        sp.dma_start(zy[:, k * SLOT:(k + 1) * SLOT],
                                     zd[0, :, k * SLOT:(k + 1) * SLOT]).then_inc(z_in[k], 16)
                iteration("head", 0)
                with sp.Fori(1, PAIRS - 1) as j:
                    iteration("body", j)
                iteration("body", PAIRS - 1, more=False)
                iteration("tail", PAIRS)

            def value(n):
                return n if isinstance(n, int) else sp.snap(sp.to_reg(n))

            def run_mix(l):
                base = mix_base(l)

                def load(c, par):
                    sp.dma_start(wb[par][:, 0:4096], w_modes[l, c]).then_inc(wx_in[par], 16)
                    for half, blk, row in ((0, 0, 0), (0, 2, 1), (1, 1, 0), (1, 0, 1)):
                        sp.dma_start(xb[par][row * C:(row + 1) * C, half * 4096:(half + 1) * 4096],
                                     ad[c, blk].rearrange("c b m -> c (b m)")).then_inc(wx_in[par], 16)

                def store(c, par):
                    sp.wait_ge(freed[3], base[3] + 2 * (c + 1))
                    sp.dma_start(md[c].rearrange("o b m -> o (b m)"),
                                 mo[par * C:(par + 1) * C, :]).then_inc(m_out[par], 16)

                z_count, a_count, squares, pairs, m_count = (
                    value(LEAD + n * (l + 1)) for n in (16 * PAIRS, 6 * 16 * PAIRS, 4 * PAIRS, PAIRS, 16 * (CH // 2)))
                for k in range(4):
                    sp.wait_ge(z_out[k], z_count)
                sp.wait_ge(a_out, a_count)
                sp.wait_ge(squared, squares)
                sp.wait_ge(z_summed, pairs)
                sp.sem_inc(arena_free, 1)
                load(0, 0)
                load(1, 1)
                with sp.Fori(0, CH // 2 - 1) as i:
                    for par in range(2):
                        store(2 * i + par, par)
                        load(2 * i + par + 2, par)
                for par in range(2):
                    store(CH - 2 + par, par)
                sp.wait_ge(norm_ready, l + 1)
                for par in range(2):
                    sp.wait_ge(m_out[par], m_count)

            load_pw(0)
            run_pass("first", 0, [LEAD] * 4)
            with sp.Fori(0, LAYERS - 1) as l:
                run_mix(l)
                load_pw(l + 1)
                run_pass("middle", l + 1, pass_base(l))
            run_mix(LAYERS - 1)
            run_pass("last", LAYERS, pass_base(LAYERS - 1))
            sp.wait_ge(t_out, LEAD + 32 * PAIRS)

            sp.wait_ge(blank, 1)
            for i in range(2):
                r = slice(i * C, (i + 1) * C)
                dst = wq_m[r].rearrange("p (h e) -> p h e", h=HEADS)[:, :, r]
                sp.dma_start(dst, wq_t.rearrange("c (h d) -> c h d", h=HEADS)).then_inc(weights_in, 16)
                sp.dma_start(wk_m[r, r], wk_t).then_inc(weights_in, 16)
                sp.dma_start(wv_m[r, r], wv_t).then_inc(weights_in, 16)
                sp.dma_start(w1_m[r, i * 2 * P:(i + 1) * 2 * P], w1).then_inc(weights_in, 16)
                sp.dma_start(wg_m[:, 8 * i:8 * i + 8], wg[i * P:(i + 1) * P, :]).then_inc(weights_in, 16)
                sp.dma_start(wd_m[:, i * 512:(i + 1) * 512], wd[i * P:(i + 1) * P, :]).then_inc(weights_in, 16)
                sp.dma_start(b1_m[:, i:i + 1], b1[i]).then_inc(weights_in, 16)
            sp.dma_start(wo_m.rearrange("p (k o) -> p k o", k=4),
                         wo_t.rearrange("(k p) o -> p k o", p=P)).then_inc(weights_in, 16)
            sp.dma_start(bd_m, bd.to_broadcast([TT, 8 * C])).then_inc(weights_in, 16)
            sp.dma_start(bg_m, bg.to_broadcast([TT, 8])).then_inc(weights_in, 16)
            sp.dma_start(tok[:, 0, :], cls_tok.to_broadcast([B, S])).then_inc(cls_out, 16)
            sp.wait_ge(cls_out, 16)

            def tokens(a):
                return [a[i * 32:(i + 1) * 32].rearrange("b t c -> (b t) c").rearrange("(n p) c -> p n c", p=TT)
                        for i in range(2)]

            tv = tokm.rearrange("p (n i c) -> p i n c", i=2, c=S)
            for i in range(2):
                sp.dma_start(tv[:, i], tokens(tok)[i]).then_inc(tok_in, 16)
            sp.wait_ge(freed[(G_V + 3) % 4], gfill(G_V + 3))
            for i in range(2):
                sp.dma_start(vd[i * 32:(i + 1) * 32].rearrange("b (o t) -> o b t", t=T),
                             vc[i * C:(i + 1) * C].rearrange("p (b t) -> p b t", t=T)).then_inc(v_out, 16)
            sp.wait_ge(v_out, 32)
            sp.dma_start(vv.rearrange("p (b d) -> p b d", d=S),
                         vd.rearrange("b (t d) -> t b d", d=S)).then_inc(v_in, 16)

            def store_context(b):
                sp.wait_ge(c_read, LEAD + b + 1)
                for i in range(2):
                    src = co[:, i * 320:(i + 1) * 320].rearrange("p (n d) -> p n d", d=S)
                    sp.dma_start(cd[b + 32 * i].rearrange("(n p d) -> p n d", p=TT, d=S), src).then_inc(c_out, 16)

            with sp.Fori(0, 32) as b:
                store_context(b)
            sp.wait_ge(c_out, LEAD + 32 * 32)
            for k in range(4):
                src = cd.rearrange("b (c t) -> c b t", t=T)[k * P:(k + 1) * P]
                sp.dma_start(ct.rearrange("p (k b t) -> p k b t", k=4, t=T)[:, k], src).then_inc(c_in, 16)
            sp.wait_ge(res_ready, 1)
            for i in range(2):
                sp.dma_start(tokens(out)[i], tv[:, i]).then_inc(res_out, 16)
            sp.wait_ge(res_out, 32)

        @block.tensor
        def _(pe):
            def turn(out_, in_):
                n = in_.shape[0]
                return pe.transpose(out_, in_, ident[0:n, 0:n])

            def three(out_, stationary, moving):
                pe.matmul(out_, stationary[0], moving[0], start=True, stop=False)
                pe.matmul(out_, stationary[0], moving[1], start=False, stop=False)
                return pe.matmul(out_, stationary[1], moving[0], start=False, stop=True)

            def parts(a, at, n):
                return [a[:, i, at:at + n] for i in range(2)]

            def run_pass(kind, q, base):
                def emptied(step, part, j):
                    pe.wait_ge(freed[SLOTS[kind][step]], fills(kind, part, j, step, base))

                def iteration(part, j):
                    for step in steps_of(kind, part):
                        slot = SLOTS[kind][step]
                        n = fills(kind, part, j, step, base)
                        o = ps[slot]
                        pe.wait_ge(freed[slot], n - 1)
                        if step == "mT":
                            pe.wait_ge(m_in, 2 * 16 * ((q - 1) * PAIRS + j + 1))
                            v = ms.rearrange("p (k y) -> p k y", y=8)
                            for i in range(8):
                                mm = turn(o[:, i * P:(i + 1) * P], v[:, :, i])
                        elif step in ("ih0", "ih1"):
                            a = int(step[2])
                            emptied("mT", part, j)
                            for i in range(4):
                                mm = three(o[:, i * 256:(i + 1) * 256], parts(mt, (4 * a + i) * P, P), eh_m)
                        elif step in ("gT0", "gT1"):
                            a = int(step[2])
                            emptied("ih1", part, j)
                            for i in range(8):
                                mm = turn(o[:, i * P:(i + 1) * P], gg[:, (8 * a + i) * P:(8 * a + i + 1) * P])
                        elif step.startswith("iw") and kind == "first":
                            k = int(step[2])
                            pe.wait_ge(x_in, 16 * (j + 1))
                            for i in range(2):
                                mm = pe.matmul(o[:, i * 512:(i + 1) * 512], fc0[:, :],
                                               zy[:, (2 * k + i) * 512:(2 * k + i + 1) * 512],
                                               start=True, stop=True)
                        elif step.startswith("iw"):
                            k = int(step[2])
                            emptied(f"gT{k // 2}", part, j)
                            for i in range(4):
                                mm = three(o[:, i * 256:(i + 1) * 256], parts(gt, (4 * k + i) * P, P), ew_m)
                        elif step.startswith("pw"):
                            k = int(step[2])
                            pe.wait_ge(h_split[k], q * PAIRS + j)
                            for i in range(2):
                                mm = three(o[:, i * 512:(i + 1) * 512], parts(pws, 0, P),
                                           parts(hs, (2 * k + i) * 512, 512))
                        elif step.startswith("hT"):
                            k = int(step[2])
                            pe.wait_ge(h_ready[k], q * PAIRS + j)
                            for i in range(8):
                                mm = turn(o[:, i * P:(i + 1) * P], hh[:, (8 * k + i) * P:(8 * k + i + 1) * P])
                        elif step in ("fw0", "fw1", "fw2", "fw3"):
                            k = int(step[2])
                            emptied(f"hT{k}", part, j)
                            for i in range(8):
                                mm = pe.matmul(o[:, i * P:(i + 1) * P],
                                               ht[:, (8 * k + i) * P:(8 * k + i + 1) * P], fw_m,
                                               start=True, stop=True)
                        elif step in ("dT0", "dT1"):
                            a = int(step[2])
                            emptied("fw3", part, j)
                            for i in range(8):
                                mm = turn(o[:, i * P:(i + 1) * P], d1[:, (8 * a + i) * P:(8 * a + i + 1) * P])
                        elif step in ("fh0", "fh1"):
                            a = int(step[2])
                            emptied(f"dT{a}", part, j)
                            for i in range(8):
                                mm = pe.matmul(o[:, i * P:(i + 1) * P],
                                               d1t[:, (8 * a + i) * P:(8 * a + i + 1) * P], fh_m,
                                               start=True, stop=True)
                        elif step.startswith("fc"):
                            i, k = divmod(int(step[2]), 4)
                            pe.wait_ge(h_split[k], q * PAIRS + j)
                            for n2 in range(2):
                                mm = three(o[:, n2 * 512:(n2 + 1) * 512], [fc1s[:, s, i, :] for s in range(2)],
                                           parts(hs, (2 * k + n2) * 512, 512))
                        elif step == "sum":
                            for r in range(16):
                                k, c = divmod(r, 2)
                                if c == 0:
                                    pe.wait_ge(g_split[k % 2], LEAD + 4 * (j - 1) + k // 2 + 1)
                                for g in (g_hi, g_lo):
                                    mm = pe.matmul(o[0:64, 0:512], fc2[:, 15 - r:79 - r], g[k][:, c * 512:(c + 1) * 512],
                                                   start=(r == 0 and g is g_hi), stop=(r == 15 and g is g_lo))
                        mm.then_inc(filled[slot], 1)

                if kind != "last":
                    pe.wait_ge(pw_split, 2 * (q + 1))
                iteration("head", 0)
                with pe.Fori(1, PAIRS) as j:
                    iteration("body", j)
                iteration("tail", PAIRS)

            def run_mix(l):
                base = mix_base(l)
                with pe.Fori(0, CH // 2) as i:
                    pe.wait_ge(pw_spread, l + 1)
                    for par in range(2):
                        pe.wait_ge(wx_in[par], 5 * 16 * (l * (CH // 2) + i + 1))
                        w = wb[par].rearrange("p (o m) -> p o m", m=MODES)
                        v = xb[par].rearrange("p (h b m) -> p h b m", h=2, m=MODES)
                        for g in range(8):
                            slot = g % 4
                            pe.wait_ge(freed[slot], base[slot] + 4 * i + 2 * par + g // 4)
                            for n in range(8):
                                y, kx = divmod(n, KC)
                                m = kx * KY + 2 * g + y
                                mm = pe.matmul(ps[slot][:, n * P:(n + 1) * P], w[:, :, m], v[:, :, :, m],
                                               start=True, stop=True)
                            mm.then_inc(filled[slot], 1)
                pe.wait_ge(stats, l + 1)
                pe.wait_ge(freed[3], base[3] + 2 * CH)
                pe.matmul(ps[3][:, 0:12], dup, st[:, :], start=True, stop=True).then_inc(filled[3], 1)

            pe.wait_ge(consts_in, 16)
            pe.wait_ge(small_in, 16 * 11)
            pe.wait_ge(fc2_ready, 2)
            run_pass("first", 0, [LEAD] * 4)
            with pe.Fori(0, LAYERS - 1) as l:
                run_mix(l)
                run_pass("middle", l + 1, pass_base(l))
            run_mix(LAYERS - 1)
            pe.wait_ge(fc2_ready, 3)
            pe.wait_ge(fc_split, 3)
            run_pass("last", LAYERS, pass_base(LAYERS - 1))

            def fill(g):
                pe.wait_ge(freed[g % 4], gfill(g) - 1)
                return ps[g % 4]

            def transposes(first, ready):
                pe.wait_ge(xn_ready, ready)
                for g in range(3):
                    o = fill(first + g)
                    for i in range(8 * g, min(8 * g + 8, TILES)):
                        at = (i % 8) // 4 * 512 + i % 4 * TT
                        mm = turn(o[:, at:at + TT], xn[:, i * P:(i + 1) * P])
                    mm.then_inc(filled[(first + g) % 4], 1)

            def project(first, weights):
                for n in range(4):
                    o = fill(first + n)
                    for i in range(2):
                        mm = pe.matmul(o[:, i * 512:i * 512 + 260], weights,
                                       xt[:, (2 * n + i) * 260:(2 * n + i + 1) * 260], start=True, stop=True)
                    mm.then_inc(filled[(first + n) % 4], 1)

            transposes(G_XT, 1)
            pe.wait_ge(weights_in, 17 * 16)
            pe.wait_ge(freed[(G_XT + 2) % 4], gfill(G_XT + 2))
            project(G_K, wk_m)
            project(G_V, wv_m)
            for h in range(HEADS):
                project(G_Q + 4 * h, wq_m[:, h * P:(h + 1) * P])

            def scores(b):
                pe.wait_ge(qb_ready, b + 1)
                if not (isinstance(b, int) and b == 0):
                    pe.wait_ge(s_read, b)
                for i in range(5):
                    at = i // 3 * 512 + i % 3 * 130
                    mm = pe.matmul(ps[0][0:TT, at:at + 130], qb[:, i * TT:(i + 1) * TT],
                                   kb[:, bass.ds(b * 130, 130)], start=True, stop=True)
                mm.then_inc(s_full, 1)

            def context(b, first=False):
                pe.wait_ge(e_ready, b + 1)
                pe.wait_ge(t_read, LEAD + b)
                for i in range(5):
                    for half in range(2):
                        n = half * 5 + i
                        o = ps[1 + n // 8][0:T, n % 8 // 4 * 512 + n % 4 * TT:n % 8 // 4 * 512 + (n % 4 + 1) * TT]
                        mm = turn(o, ex[:, (2 * i + half) * T:(2 * i + half + 1) * T])
                mm.then_inc(t_full, 1)
                pe.wait_ge(t_read, LEAD + b + 1)
                pe.wait_ge(c_read, LEAD + b)
                for half in range(2):
                    for i in range(5):
                        mm = pe.matmul(ps[3][0:TT, half * 512 + i * S:half * 512 + (i + 1) * S],
                                       attn_t[:, (half * 5 + i) * TT:(half * 5 + i + 1) * TT],
                                       vv[:, bass.ds((half * 32 + b) * S, S)], start=True, stop=True)
                mm.then_inc(c_full, 1)

            for g in range(G_WO - 4, G_WO):
                pe.wait_ge(freed[g % 4], gfill(g))
            pe.wait_ge(v_in, 16)
            scores(0)
            with pe.Fori(1, 32) as b:
                scores(b)
                context(b - 1)
            context(31)

            pe.wait_ge(c_in, 64)
            pe.wait_ge(c_read, LEAD + 32)
            for g in range(3):
                o = fill(G_WO + g)
                for n in range(16 * g, min(16 * g + 16, 40)):
                    i, half = divmod(n, 2)
                    for k in range(4):
                        at = k * 2 * HALF + half * HALF + i * TT
                        mm = pe.matmul(o[0:TT, n % 16 * S:(n % 16 + 1) * S], ct[:, at:at + TT],
                                       wo_m[:, k * S:(k + 1) * S], start=(k == 0), stop=(k == 3))
                mm.then_inc(filled[(G_WO + g) % 4], 1)
            transposes(G_XT2, 2)
            pe.wait_ge(freed[(G_XT2 + 2) % 4], gfill(G_XT2 + 2))
            for g in range(10):
                o = fill(G_H + g)
                for u in range(2 * g, 2 * g + 2):
                    hc, rest = divmod(u, 10)
                    half, n = divmod(rest, 5)
                    w = w1_m[:, half * 2 * P + hc * P:half * 2 * P + (hc + 1) * P]
                    mm = pe.matmul(o[:, u % 2 * 512:u % 2 * 512 + 416], w, xt[:, n * 416:(n + 1) * 416],
                                   start=True, stop=True)
                mm.then_inc(filled[(G_H + g) % 4], 1)

            def hidden(n, hc):
                i, half = divmod(n, 2)
                at = (hc * 2 + half) * HALF + i * TT
                return hid[:, at:at + TT]

            o = fill(G_LG)
            pe.wait_ge(freed[(G_H + 9) % 4], gfill(G_H + 9))
            for n in range(40):
                for hc in range(2):
                    mm = pe.matmul(o[0:TT, n * 8:n * 8 + 8], hidden(n, hc), wg_m[:, hc * 8:hc * 8 + 8],
                                   start=(hc == 0), stop=(hc == 1))
            mm.then_inc(filled[G_LG % 4], 1)
            for g in range(20):
                o = fill(G_Y + g)
                for i in range(2):
                    for hc in range(2):
                        mm = pe.matmul(o[0:TT, i * 512:(i + 1) * 512], hidden(2 * g + i, hc),
                                       wd_m[:, hc * 512:(hc + 1) * 512], start=(hc == 0), stop=(hc == 1))
                mm.then_inc(filled[(G_Y + g) % 4], 1)

        @block.vector
        def _(dve):
            def run_pass(kind, q, base):
                def iteration(part, j):
                    for step in steps_of(kind, part):
                        slot = SLOTS[kind][step]
                        n = fills(kind, part, j, step, base)
                        o = ps[slot]
                        k = quarter(step)
                        cols = slice(k * SLOT, (k + 1) * SLOT)
                        if step.startswith("hT"):
                            dve.wait_ge(filled[slot], n)
                            dve.tensor_copy(ht[:, cols], o[:, :]).then_inc(freed[slot], 1)
                        elif step.startswith("dT"):
                            dve.wait_ge(filled[slot], n)
                            dve.tensor_copy(d1t[:, cols], o[:, :]).then_inc(freed[slot], 1)
                        elif step == "mT" or step.startswith("gT"):
                            turn = ["mT", "gT0", "gT1"].index(step)
                            dst = mt if step == "mT" else gt[:, :, cols]
                            dve.wait_ge(hi_taken, 3 * ((q - 1) * PAIRS + j) + turn + 1)
                            dve.tensor_tensor(dst[:, 1], o[:, :], dst[:, 0], ALU.subtract).then_inc(freed[slot], 1)
                        elif step.startswith("iw") and kind == "first":
                            dve.wait_ge(filled[slot], n)
                            dve.wait_ge(h_ready[k], q * PAIRS + j)
                            dve.tensor_copy(y0[:, cols], o[:, :]).then_inc(freed[slot], 1)
                        elif step.startswith("iw"):
                            dve.wait_ge(z_in[k], 16 * ((q - 1) * PAIRS + j + 1))
                            dve.wait_ge(filled[slot], n)
                            dve.tensor_tensor(zy[:, cols], o[:, :], zy[:, cols], ALU.add)\
                                .then_inc(freed[slot], 1)
                        elif step.startswith("pw"):
                            dve.wait_ge(z_out[k], LEAD + 16 * (q * PAIRS + j - 1))
                            dve.wait_ge(squared, LEAD + 4 * (q * PAIRS + j - 1))
                            dve.wait_ge(filled[slot], n)
                            dve.tensor_copy(zo[:, cols], o[:, :]).then_inc(freed[slot], 1)
                        elif step == "sum":
                            dve.wait_ge(t_out, LEAD + 32 * (j - 1))
                            dve.wait_ge(ot_ready, j)
                            dve.tensor_tensor(ot, o[0:16, 0:512], ot_lo, ALU.add).then_inc(freed[slot], 1)
                        if step.startswith("iw") and k > 0:
                            round_h(part, j, k - 1)
                        if step.startswith("fc") and step != "fc0":
                            split_hidden(j, int(step[2]) - 1)
                        if step == "iw2" and kind == "last" and part == "body" or step == "fc7" and part == "tail":
                            split_hidden(j, 7)
                        if step == "dT1" and part == "body" or step == steps_of(kind, part)[-1] and (
                                part == "head" or part == "body" and kind == "last"):
                            round_h(part, j, 3)

                def round_h(part, j, k):
                    last_reader = f"fc{4 + k}" if kind == "last" else f"pw{k}"
                    dve.wait_ge(h_ready[k], q * PAIRS + j + 1)
                    if part == "body":
                        slot = SLOTS[kind][last_reader]
                        dve.wait_ge(filled[slot], fills(kind, part, j, last_reader, base))
                    dve.tensor_copy(hs[:, 0, k * SLOT:(k + 1) * SLOT], hh[:, k * SLOT:(k + 1) * SLOT])\
                        .then_inc(h_hi, 1)

                def split_hidden(j, k):
                    step = f"fc{k}"
                    slot = SLOTS[kind][step]
                    dve.wait_ge(freed[slot], fills(kind, "body" if not isinstance(j, int) else "tail", j, step, base))
                    dve.wait_ge(filled[SLOTS[kind]["sum"]], once_before(kind, j, "sum", base))
                    dve.tensor_copy(g_hi[k], gf[k % 2]).then_inc(g_rounded, 1)
                    if k % 2:
                        dve.wait_ge(g_rounded, 8 * (j - 1) + k + 1)
                        dve.tensor_tensor(g_lo[k], gf[1], g_hi[k], ALU.subtract).then_inc(g_split[1], 1)

                if kind != "last":
                    dve.wait_ge(pw_in, 2 * 16 * (q + 1))
                    dve.tensor_copy(pws[:, 0], pwt[:, :]).then_inc(pw_split, 1)
                    dve.wait_ge(pw_split, 2 * q + 1)
                    dve.tensor_tensor(pws[:, 1], pwt[:, :], pws[:, 0], ALU.subtract).then_inc(pw_split, 1)
                iteration("head", 0)
                with dve.Fori(1, PAIRS) as j:
                    iteration("body", j)
                iteration("tail", PAIRS)

            def run_mix(l):
                base = mix_base(l)
                dve.wait_ge(arena_free, l + 1)
                dve.wait_ge(pw_in, 2 * 16 * (l + 1))
                for par in range(2):
                    w = wb[par][:, 4096:8192].rearrange("p (o m) -> p o m", m=MODES)
                    dve.memset(w[C:P], 0.0)
                    last = dve.tensor_scalar(w[0:C], pwt[0:C, 0:C].unsqueeze(2).to_broadcast([C, C, MODES]),
                                             2.0, None, ALU.mult)
                last.then_inc(pw_spread, 1)
                with dve.Fori(0, CH // 2) as i:
                    for par in range(2):
                        m = mo[par * C:(par + 1) * C, :].rearrange("p (b k y) -> p b y k", b=B, y=KY)
                        for g in range(8):
                            slot = g % 4
                            dve.wait_ge(m_taken, 8 * ((l * (CH // 2) + i) * 2 + par) + g + 1)
                            if par == 0 and g == 0:
                                dve.tensor_reduce(zdc[C:P, bass.ds(i, 1)], ps[slot][C:P, 0:B], AX.X, ALU.add)
                            for y in range(2):
                                col = slice(slot * SLOT + y * 512, slot * SLOT + (y + 1) * 512)
                                z = ps[slot][C:P, y * 512:(y + 1) * 512].rearrange("p (k b) -> p b k", b=B)
                                last = dve.tensor_tensor_reduce(
                                    mjunk[C:P, col].rearrange("p (b k) -> p b k", b=B), z, m[:, :, 2 * g + y],
                                    1.0, 0.0, ALU.mult, ALU.add, eacc[C:P, par, 2 * g + y:2 * g + y + 1])
                            last.then_inc(freed[slot], 1)

                chain = [l * N_STATS]

                def link(ins):
                    chain[0] = chain[0] + 1
                    ins.then_inc(stats_chain, 1)
                    dve.wait_ge(stats_chain, chain[0])

                start = chain[0]
                dve.wait_ge(e_summed, LEAD + (CH // 2) * (l + 1))
                dve.wait_ge(z_summed, LEAD + PAIRS * (l + 1))
                link(dve.memset(st[:, :], 0.0))
                link(dve.tensor_reduce(st[:, 0:1], zsum[:, :], AX.X, ALU.add))
                link(dve.tensor_reduce(st[0:C, 1:2], esum[0:C, :, 1:KY], AX.XY, ALU.add))
                link(dve.tensor_reduce(st[0:C, 2:3], esum[0:C, :, 0], AX.X, ALU.add))
                link(dve.tensor_reduce(st[C:P, 3:4], esum[C:P, :, 1:KY], AX.XY, ALU.add))
                link(dve.tensor_reduce(st[C:P, 4:5], esum[C:P, :, 0], AX.X, ALU.add))
                for k in range(1, KX // 2):
                    link(dve.tensor_tensor(xp[:, (k - 1) * P:k * P], m0[:, k * P:(k + 1) * P],
                                           m0[:, (KX - k) * P:(KX - k + 1) * P], ALU.mult))
                v = xp.rearrange("p (k r b) -> p r k b", r=2, b=B)
                link(dve.tensor_reduce(st[0:C, 5:6], v[:, 0], AX.XY, ALU.add))
                link(dve.tensor_reduce(st[0:C, 6:7], v[:, 1], AX.XY, ALU.add))
                link(dve.tensor_tensor(xp[:, 0:P], m0[:, 0:P], m0[:, 0:P], ALU.mult))
                link(dve.tensor_reduce(st[0:C, 7:8], xp[:, 0:B], AX.X, ALU.add))
                link(dve.tensor_reduce(st[0:C, 8:9], xp[:, B:P], AX.X, ALU.add))
                link(dve.tensor_reduce(st[0:C, 9:10], m0[:, 0:B], AX.X, ALU.add))
                link(dve.tensor_copy(st[C:P, 10:11], zdc[C:P, 0:1]))
                dve.memset(zsum[:, :], 0.0)
                dve.memset(esum[:, :, :], 0.0)
                dve.memset(tmp[:, 0, 0:1], 0.0).then_inc(stats, 1)
                dve.wait_ge(filled[3], base[3] + 2 * CH + 1)
                link(dve.tensor_tensor(tmp[:, 0, :], ps[3][:, 0:12], const("sq"), ALU.mult))
                dve.tensor_tensor(tmp[:, 1, :], ps[3][:, 0:12], const("av"), ALU.mult).then_inc(freed[3], 1)
                dve.wait_ge(freed[3], base[3] + 2 * CH + 1)
                link(dve.tensor_reduce(mom[:, 0:2], tmp[:, :, :], AX.X, ALU.add))
                sq, mean = mom[:, 0:1], mom[:, 1:2]
                link(dve.tensor_tensor(mom[:, 2:3], mean, mean, ALU.mult))
                link(dve.tensor_tensor(mom[:, 3:4], sq, mom[:, 2:3], ALU.subtract))
                dve.tensor_scalar(mom[:, 4:5], mom[:, 3:4], 0.0, EPS, ALU.max, ALU.add).then_inc(root, 1)
                dve.wait_ge(root, 2 * (l + 1))
                link(dve.reciprocal(mom[:, 6:7], mom[:, 5:6]))
                link(dve.tensor_tensor(mom[:, 7:8], mom[:, 6:7], mom[:, 6:7], ALU.mult))
                link(dve.tensor_tensor(mom[:, 7:8], mom[:, 7:8], mom[:, 4:5], ALU.mult))
                link(dve.tensor_scalar(mom[:, 7:8], mom[:, 7:8], -0.5, 1.5, ALU.mult, ALU.add))
                link(dve.tensor_tensor(mom[:, 6:7], mom[:, 7:8], mom[:, 6:7], ALU.mult))
                layer = chn[:, bass.ds(l, 1), :] if not isinstance(l, int) else chn[:, l:l + 1, :]
                link(dve.tensor_copy(cur[:, :].unsqueeze(1), layer))
                gamma, beta, pwb = (cur[:, i:i + 1] for i in range(3))
                link(dve.tensor_tensor(scale_v, gamma, mom[:, 6:7], ALU.mult))
                link(dve.tensor_tensor(mom[:, 10:11], mean, pwb, ALU.add))
                link(dve.tensor_tensor(mom[:, 10:11], pwb, mom[:, 10:11], ALU.subtract))
                link(dve.tensor_tensor(mom[:, 10:11], mom[:, 10:11], scale_v, ALU.mult))
                dve.tensor_tensor(shift_v, mom[:, 10:11], beta, ALU.add).then_inc(norm_ready, 1)
                n = chain[0] - start
                assert not isinstance(l, int) or n == N_STATS, n

            dve.memset(pwt[:, :], 0.0)
            dve.memset(fc0[:, :], 0.0)
            dve.memset(fc1[:, :, :], 0.0)
            dve.memset(fc2[:, :].bitcast(F32), 0.0)
            dve.memset(zdc[:, :], 0.0)
            dve.memset(zsum[:, :], 0.0)
            dve.memset(esum[:, :, :], 0.0)
            dve.memset(eacc[:, :, :], 0.0)
            dve.memset(zy[:, :], 0.0).then_inc(zeroed, 1)
            dve.wait_ge(zeroed, 1)
            dve.wait_ge(small_in, 16 * 11)
            dve.wait_ge(consts_in, 16)
            dve.tensor_copy(inv_s[:, 0], inv_m).then_inc(fc2_ready, 1)
            dve.wait_ge(fc2_ready, 1)
            dve.tensor_tensor(inv_s[:, 1], inv_m, inv_s[:, 0], ALU.subtract).then_inc(fc2_ready, 1)
            dve.tensor_copy(fc2[:, 15:16], fc2c[:, :]).then_inc(fc_split, 1)
            dve.wait_ge(fc_split, 1)
            dve.tensor_tensor(fc2[:, 47:48], fc2c[:, :], fc2[:, 15:16], ALU.subtract).then_inc(fc_split, 1)
            dve.wait_ge(fc_split, 2)
            dve.tensor_copy(fc1s[:, 0], fc1[:, :, :]).then_inc(fc2_ready, 1)
            dve.wait_ge(fc2_ready, 3)
            dve.tensor_tensor(fc1s[:, 1], fc1[:, :, :], fc1s[:, 0], ALU.subtract).then_inc(fc_split, 1)
            run_pass("first", 0, [LEAD] * 4)
            with dve.Fori(0, LAYERS - 1) as l:
                run_mix(l)
                run_pass("middle", l + 1, pass_base(l))
            run_mix(LAYERS - 1)
            run_pass("last", LAYERS, pass_base(LAYERS - 1))

            links = [0]

            def link(ins):
                links[0] = links[0] + 1
                ins.then_inc(link_t, 1)
                dve.wait_ge(link_t, links[0])

            dve.wait_ge(t_out, LEAD + 32 * PAIRS)
            for m in (kb, wq_m, wk_m, wv_m):
                dve.memset(m, 0.0)
            dve.memset(w1_m, 0.0).then_inc(blank, 1)

            def rows(a):
                return a.rearrange("p (n c) -> p n c", c=S)

            def wide(a, n=S):
                return a.unsqueeze(2).to_broadcast([TT, a.shape[1], n])

            def norm(turn):
                link(dve.tensor_reduce(red, rows(tokm), AX.X, ALU.add))
                link(dve.tensor_scalar(mean_t, red, 1.0 / S, None, ALU.mult))
                link(dve.tensor_tensor(rows(xn), rows(tokm), wide(mean_t), ALU.subtract))
                link(dve.tensor_tensor(lnw, xn, xn, ALU.mult))
                link(dve.tensor_reduce(red, rows(lnw), AX.X, ALU.add))
                dve.tensor_scalar(var_t, red, 1.0 / S, EPS, ALU.mult, ALU.add).then_inc(ln_root, 1)
                dve.wait_ge(ln_root, 2 * turn)
                link(dve.reciprocal(inv_t, rt_t))
                link(dve.tensor_tensor(nw_t, inv_t, inv_t, ALU.mult))
                link(dve.tensor_tensor(nw_t, nw_t, var_t, ALU.mult))
                link(dve.tensor_scalar(nw_t, nw_t, -0.5, 1.5, ALU.mult, ALU.add))
                link(dve.tensor_tensor(inv_t, inv_t, nw_t, ALU.mult))
                dve.tensor_tensor(rows(xn), rows(xn), wide(inv_t), ALU.mult).then_inc(xn_ready, 1)

            def transposed(first):
                for g in range(3):
                    dve.wait_ge(filled[(first + g) % 4], gfill(first + g))
                    n = 2 if g < 2 else 1
                    src = ps[(first + g) % 4][:, 0:n * 512].rearrange("p (k c) -> p k c", k=n)[:, :, 0:416]
                    dve.tensor_copy(xt[:, g * 832:g * 832 + n * 416].rearrange("p (k c) -> p k c", k=n), src)\
                        .then_inc(freed[(first + g) % 4], 1)

            def pair(g, n=260):
                return ps[g % 4][:, :].rearrange("p (k c) -> p k c", k=2)[:, :, 0:n]

            dve.wait_ge(tok_in, 32)
            norm(1)
            transposed(G_XT)
            for g in range(G_V, G_V + 4):
                dve.wait_ge(filled[g % 4], gfill(g))
                n = g - G_V
                dve.tensor_copy(vc[:, n * 520:(n + 1) * 520].rearrange("p (k c) -> p k c", k=2), pair(g))\
                    .then_inc(freed[g % 4], 1)
            for g in range(G_Q + 1, G_Q + 32, 2):
                dve.wait_ge(filled[g % 4], gfill(g))
                h, n = divmod(g - G_Q, 4)
                dst = qt.rearrange("p (t h) -> p t h", h=HEADS)[:, n * 520:(n + 1) * 520, h]
                dve.tensor_copy(dst.rearrange("p (k c) -> p k c", k=2), pair(g)).then_inc(freed[g % 4], 1)

            start = links[0]
            N_LOOP = 3

            def softmax(b):
                dve.wait_ge(s_full, LEAD + b + 1)
                for a, e in ((0, 3), (3, 5)):
                    v = ps[0][0:TT, a // 3 * 512:a // 3 * 512 + (e - a) * 130].rearrange("p (n t) -> p n t", t=T)
                    last = dve.tensor_reduce(mx[:, 2 * a:2 * e], v, AX.X, ALU.max)
                link(last)
                for a, e in ((0, 3), (3, 5)):
                    v = ps[0][0:TT, a // 3 * 512:a // 3 * 512 + (e - a) * 130].rearrange("p (n t) -> p n t", t=T)
                    d = ss[:, 2 * a * T:2 * e * T].rearrange("p (n t) -> p n t", t=T)
                    last = dve.tensor_tensor(d, v, wide(mx[:, 2 * a:2 * e], T), ALU.subtract)
                last.then_inc(s_read, 1)

            def sums(b):
                dve.wait_ge(e_ready, b + 1)
                link(dve.tensor_reduce(sm, ex.rearrange("p (n t) -> p n t", t=T), AX.X, ALU.add))
                link(dve.reciprocal(rc, sm))

            def normalise(b):
                dve.wait_ge(c_full, LEAD + b + 1)
                dve.wait_ge(c_out, LEAD + 32 * b)
                for half in range(2):
                    src = ps[3][0:TT, half * 512:half * 512 + 320].rearrange("p (n d) -> p n d", d=S)
                    dst = co[:, half * 320:(half + 1) * 320].rearrange("p (n d) -> p n d", d=S)
                    r = rc.rearrange("p (n h) -> p h n", h=2)[:, half]
                    last = dve.tensor_tensor(dst, src, wide(r), ALU.mult)
                last.then_inc(c_read, 1)

            softmax(0)
            sums(0)
            after_first = links[0]
            with dve.Fori(1, 32) as b:
                links[0] = (b - 1) * N_LOOP + after_first
                softmax(b)
                normalise(b - 1)
                dve.wait_ge(c_read, LEAD + b)
                sums(b)
            links[0] = after_first + 31 * N_LOOP
            normalise(31)

            for g in range(3):
                dve.wait_ge(filled[(G_WO + g) % 4], gfill(G_WO + g))
                a, e = g * SLOT, min((g + 1) * SLOT, 2560)
                dve.tensor_tensor(tokm[:, a:e], ps[(G_WO + g) % 4][0:TT, 0:e - a], tokm[:, a:e], ALU.add)\
                    .then_inc(freed[(G_WO + g) % 4], 1)
            dve.wait_ge(freed[(G_WO + 2) % 4], gfill(G_WO + 2))
            norm(2)
            transposed(G_XT2)

            def by_token(a):
                return a.rearrange("p (n e) -> p n e", e=8)

            dve.wait_ge(filled[G_LG % 4], gfill(G_LG))
            dve.tensor_tensor(by_token(lg), by_token(ps[G_LG % 4][0:TT, 0:320]),
                              bg_m.unsqueeze(1).to_broadcast([TT, 40, 8]), ALU.add).then_inc(freed[G_LG % 4], 1)
            dve.wait_ge(freed[G_LG % 4], gfill(G_LG))
            link(dve.tensor_reduce(red, by_token(lg), AX.X, ALU.max))
            dve.tensor_tensor(by_token(lg), by_token(lg), wide(red, 8), ALU.subtract).then_inc(g_exp, 1)
            dve.wait_ge(g_exp, 2)
            link(dve.tensor_reduce(red, by_token(gate), AX.X, ALU.add))
            link(dve.reciprocal(inv_t, red))
            link(dve.tensor_reduce(red, by_token(gate), AX.X, ALU.max))
            link(dve.tensor_tensor(by_token(eq), by_token(gate), wide(red, 8), ALU.is_equal))
            link(dve.tensor_tensor(by_token(eq), by_token(eq),
                                   const("first")[0:TT].unsqueeze(1).to_broadcast([TT, 40, 8]), ALU.mult))
            link(dve.tensor_reduce(red, by_token(eq), AX.X, ALU.max))
            link(dve.tensor_tensor(by_token(eq), by_token(eq), wide(red, 8), ALU.is_equal))
            link(dve.tensor_tensor(by_token(gate), by_token(gate), wide(inv_t, 8), ALU.mult))
            link(dve.tensor_tensor(gate, gate, eq, ALU.mult))
            for g in range(20):
                y = yb[g % 2]
                yv = y.rearrange("p (n e c) -> p n e c", n=2, c=C)
                dve.wait_ge(filled[(G_Y + g) % 4], gfill(G_Y + g))
                for i in range(2):
                    last = dve.tensor_tensor(y[:, i * 512:(i + 1) * 512], ps[(G_Y + g) % 4][0:TT, i * 512:(i + 1) * 512],
                                             bd_m, ALU.add)
                last.then_inc(freed[(G_Y + g) % 4], 1)
                dve.wait_ge(freed[(G_Y + g) % 4], gfill(G_Y + g))
                for i in range(2):
                    gt_i = by_token(gate)[:, 2 * g + i]
                    last = dve.tensor_tensor(yv[:, i], yv[:, i], wide(gt_i, C), ALU.mult)
                link(last)
                link(dve.tensor_reduce(rows(xn)[:, 2 * g:2 * g + 2], yv.rearrange("p n e c -> p n c e"),
                                       AX.X, ALU.add))
            dve.tensor_tensor(tokm, tokm, xn, ALU.add).then_inc(res_ready, 1)

        @block.scalar
        def _(act):
            def run_pass(kind, q, base):
                def iteration(part, j):
                    for step in steps_of(kind, part):
                        slot = SLOTS[kind][step]
                        n = fills(kind, part, j, step, base)
                        o = ps[slot]
                        k = quarter(step)
                        cols = slice(k * SLOT, (k + 1) * SLOT)
                        if step in ("fw0", "fw1", "fw2", "fw3"):
                            act.wait_ge(filled[slot], n)
                            dst = d1.rearrange("p (y t x) -> p t y x", y=KY, x=4)[:, 8 * k:8 * k + 8]
                            src = o[:, :].rearrange("p (t c) -> p t c", t=8)[:, :, 0:64]
                            act.copy(dst, src.rearrange("p t (y x) -> p t y x", x=4)).then_inc(freed[slot], 1)
                        elif step in ("fh0", "fh1"):
                            act.wait_ge(a_out, LEAD + 6 * 16 * (q * PAIRS + j - 1))
                            act.wait_ge(filled[slot], n)
                            dst = d2.rearrange("p (m y) -> p y m", y=KY)[:, 8 * k:8 * k + 8]
                            src = o[:, :].rearrange("p (y m) -> p y m", y=8)[:, :, 0:96]
                            act.copy(dst, src).then_inc(freed[slot], 1)
                        elif step == "mT":
                            act.wait_ge(filled[slot], n)
                            act.copy(mt[:, 0], o[:, :]).then_inc(hi_taken, 1)
                        elif step.startswith("gT"):
                            act.wait_ge(filled[slot], n)
                            act.copy(gt[:, 0, cols], o[:, :]).then_inc(hi_taken, 1)
                        elif step.startswith("ih"):
                            act.wait_ge(filled[slot], n)
                            dst = gg.rearrange("p (h y x) -> p y h x", y=8, x=4)[:, 4 * k:4 * k + 4]
                            act.copy(dst, o[:, :].rearrange("p (y h x) -> p y h x", y=4, x=4))\
                                .then_inc(freed[slot], 1)
                        elif step.startswith("iw"):
                            act.wait_ge(freed[slot], n)
                            if kind == "first":
                                act.activation(hh[:, cols], y0[:, cols], ACT.Identity, bias=vec[:, 0:1])\
                                    .then_inc(h_ready[k], 1)
                            else:
                                act.activation(hh[:, cols], zy[:, cols], ACT.Gelu, bias=shift_v,
                                               scale=scale_v).then_inc(h_ready[k], 1)
                        elif step.startswith("pw"):
                            act.wait_ge(freed[slot], n)
                            act.wait_ge(z_summed, LEAD + q * PAIRS + j - 1)
                            act.activation(junk[:, cols], zo[:, cols], ACT.Square,
                                           accum_out=zacc[:, k:k + 1]).then_inc(squared, 1)
                        elif step.startswith("fc"):
                            e = int(step[2])
                            act.wait_ge(g_split[e % 2], LEAD + 4 * (j - 1) + e // 2)
                            act.wait_ge(filled[slot], n)
                            act.activation(gf[e % 2], o[:, :], ACT.Gelu, bias=vec[:, 1:2]).then_inc(freed[slot], 1)
                        elif step == "sum":
                            act.wait_ge(freed[slot], once_before(kind, j, "sum", base))
                            act.wait_ge(filled[slot], n)
                            act.activation(ot_lo, o[32:48, 0:512], ACT.Identity, bias=vec[32:48, 2:3])\
                                .then_inc(ot_ready, 1)

                if kind not in ("first",):
                    act.wait_ge(norm_ready, q)
                iteration("head", 0)
                with act.Fori(1, PAIRS) as j:
                    iteration("body", j)
                iteration("tail", PAIRS)

            def run_mix(l):
                base = mix_base(l)
                act.wait_ge(arena_free, l + 1)
                with act.Fori(0, CH // 2) as i:
                    act.wait_ge(e_summed, LEAD + l * (CH // 2) + i)
                    for par in range(2):
                        act.wait_ge(m_out[par], LEAD + 16 * (l * (CH // 2) + i))
                        for g in range(8):
                            slot = g % 4
                            act.wait_ge(filled[slot], base[slot] + 4 * i + 2 * par + g // 4 + 1)
                            src = ps[slot][0:C, :].rearrange("p (y k b) -> p b y k", b=B, y=2)
                            dst = mo[par * C:(par + 1) * C, :].rearrange("p (b k y) -> p b y k", b=B, y=KY)
                            act.copy(dst[:, :, 2 * g:2 * g + 2], src)
                            if g == 0:
                                act.copy(m0[:, bass.ds((2 * i + par) * 512, 512)], ps[slot][0:C, 0:512])
                            for a, e, col in ([(0, 8, 0), (8, 16, 1)] if g == 0 else [(0, 16, 2 * g)]):
                                last = act.activation(mjunk[0:C, slot * SLOT + a * B:slot * SLOT + e * B],
                                                      ps[slot][0:C, a * B:e * B], ACT.Square,
                                                      accum_out=eacc[0:C, par, col:col + 1])
                            last.then_inc(m_taken, 1)
                act.wait_ge(root, 2 * l + 1)
                act.activation(mom[:, 5:6], mom[:, 4:5], ACT.Sqrt).then_inc(root, 1)

            act.wait_ge(small_in, 16 * 11)
            run_pass("first", 0, [LEAD] * 4)
            with act.Fori(0, LAYERS - 1) as l:
                run_mix(l)
                run_pass("middle", l + 1, pass_base(l))
            run_mix(LAYERS - 1)
            run_pass("last", LAYERS, pass_base(LAYERS - 1))

            act.wait_ge(ln_root, 1)
            act.activation(rt_t, var_t, ACT.Sqrt).then_inc(ln_root, 1)
            act.wait_ge(blank, 1)

            def pair(g, n=260):
                return ps[g % 4][:, :].rearrange("p (k c) -> p k c", k=2)[:, :, 0:n]

            for g in range(G_K, G_K + 4):
                act.wait_ge(filled[g % 4], gfill(g))
                n = g - G_K
                for half in range(2):
                    r = slice(half * C, (half + 1) * C)
                    dst = kb[r].rearrange("p (b h t) -> p h b t", h=2, t=T)[:, half, 8 * n:8 * n + 8]
                    for k in range(2):
                        last = act.copy(dst[:, 4 * k:4 * k + 4],
                                        pair(g)[r, k].rearrange("p (b t) -> p b t", t=T))
                last.then_inc(freed[g % 4], 1)
            for g in range(G_Q, G_Q + 32, 2):
                act.wait_ge(filled[g % 4], gfill(g))
                h, n = divmod(g - G_Q, 4)
                dst = qt.rearrange("p (t h) -> p t h", h=HEADS)[:, n * 520:(n + 1) * 520, h]
                act.copy(dst.rearrange("p (k c) -> p k c", k=2), pair(g)).then_inc(freed[g % 4], 1)

            def exponentials(b):
                act.wait_ge(s_read, b + 1)
                act.activation(ex, ss, ACT.Exp, scale=1.0 / np.sqrt(8.0)).then_inc(e_ready, 1)

            def turned(b):
                act.wait_ge(t_full, b + 1)
                act.wait_ge(c_full, LEAD + b)
                act.copy(attn_t[:, 0:832].rearrange("p (k c) -> p k c", k=2),
                         ps[1][0:T, :].rearrange("p (k c) -> p k c", k=2)[:, :, 0:416])
                act.copy(attn_t[:, 832:1040], ps[2][0:T, 0:208]).then_inc(t_read, 1)

            exponentials(0)
            with act.Fori(1, 32) as b:
                turned(b - 1)
                exponentials(b)
            turned(31)
            act.wait_ge(ln_root, 3)
            act.activation(rt_t, var_t, ACT.Sqrt).then_inc(ln_root, 1)
            for g in range(G_H, G_H + 10):
                act.wait_ge(filled[g % 4], gfill(g))
                n, hc = g - G_H, (g - G_H) // 5
                act.activation(hid[:, n * 832:(n + 1) * 832].rearrange("p (k c) -> p k c", k=2), pair(g, 416),
                               ACT.Gelu, bias=b1_m[:, hc:hc + 1]).then_inc(freed[g % 4], 1)
            act.wait_ge(g_exp, 1)
            act.activation(gate, lg, ACT.Exp).then_inc(g_exp, 1)

        @block.gpsimd
        def _(pool):
            def run_pass(kind, q, base):
                def iteration(part, j):
                    for step in steps_of(kind, part):
                        k = quarter(step)
                        cols = slice(k * SLOT, (k + 1) * SLOT)
                        if step.startswith("iw"):
                            pool.wait_ge(h_hi, 4 * (q * PAIRS + j) + k + 1)
                            pool.tensor_tensor(hs[:, 1, cols], hh[:, cols], hs[:, 0, cols], ALU.subtract)\
                                .then_inc(h_split[k], 1)
                        elif step.startswith("fc") and int(step[2]) % 2 == 0:
                            e = int(step[2])
                            pool.wait_ge(g_rounded, 8 * (j - 1) + e + 1)
                            pool.tensor_tensor(g_lo[e], gf[0], g_hi[e], ALU.subtract).then_inc(g_split[0], 1)
                        elif step == "pw3":
                            pool.wait_ge(squared, LEAD + 4 * (q * PAIRS + j))
                            pool.wait_ge(z_summed, LEAD + q * PAIRS + j - 1)
                            pool.tensor_tensor(zsum[:, :], zsum[:, :], zacc[:, :], ALU.add).then_inc(z_summed, 1)

                pool.wait_ge(zeroed, 1)
                if not (isinstance(q, int) and q == 0):
                    pool.wait_ge(norm_ready, q)
                iteration("head", 0)
                with pool.Fori(1, PAIRS) as j:
                    iteration("body", j)
                iteration("tail", PAIRS)

            def run_mix(l):
                base = mix_base(l)
                with pool.Fori(0, CH // 2) as i:
                    pool.wait_ge(freed[3], base[3] + 4 * (i + 1))
                    pool.wait_ge(e_summed, LEAD + l * (CH // 2) + i)
                    pool.tensor_tensor(esum[:, :, :], esum[:, :, :], eacc[:, :, :], ALU.add)\
                        .then_inc(e_summed, 1)

            run_pass("first", 0, [LEAD] * 4)
            with pool.Fori(0, LAYERS - 1) as l:
                run_mix(l)
                run_pass("middle", l + 1, pass_base(l))
            run_mix(LAYERS - 1)
            run_pass("last", LAYERS, pass_base(LAYERS - 1))

            for g in range(G_WO - 4, G_WO):
                pool.wait_ge(freed[g % 4], gfill(g))
            with pool.Fori(0, 32) as b:
                pool.wait_ge(s_full, LEAD + b)
                pool.tensor_copy(qb, qt[:, bass.ds(b * 520, 520)]).then_inc(qb_ready, 1)


NAMES = ["x_p", "cls_tok", "fc0_w", "fc0_b", "w_modes", "pw_t", "chan", "fc1_w", "fc1_b", "fc2_w", "fc2_b",
         "wq_t", "wk_t", "wv_t", "wo_t", "w1", "b1", "wg", "bg", "wd", "bd", "consts"]


def layout(t):
    def c(a):
        return np.ascontiguousarray(a)

    t = {k.replace("L0_", ""): np.asarray(v) for k, v in t.items()}
    x = t["x"].reshape(PAIRS, 2, PIX, 3).transpose(0, 1, 3, 2).reshape(PAIRS, 6, PIX)
    w = np.stack([np.stack([t["tok_w1r"], t["tok_w2r"]]), np.stack([t["tok_w1i"], t["tok_w2i"]])])
    w = w.reshape(2, 2, LAYERS, C, C, CH // 2, MODES)
    w = w.transpose(2, 1, 5, 0, 3, 4, 6).reshape(LAYERS, CH, P, C * MODES)
    chan = np.stack([t["tok_gamma"], t["tok_beta"], t["tok_pw_b"]], axis=-1).transpose(1, 0, 2)
    return {
        "x_p": c(x), "cls_tok": c(t["cls_tok"].reshape(1, S)), "fc0_w": c(t["tok_fc0_w"]),
        "fc0_b": c(t["tok_fc0_b"].reshape(C, 1)), "w_modes": c(w), "pw_t": c(t["tok_pw_w"].transpose(0, 2, 1)),
        "chan": c(chan), "fc1_w": c(t["tok_fc1_w"]), "fc1_b": c(t["tok_fc1_b"].reshape(HID, 1)),
        "fc2_w": c(t["tok_fc2_w"]), "fc2_b": c(t["tok_fc2_b"].reshape(1, 1)),
        "wq_t": c(t["attn_Wq"].T), "wk_t": c(t["attn_Wk"].T), "wv_t": c(t["attn_Wv"].T), "wo_t": c(t["attn_Wo"].T),
        "w1": c(t["ffn_W1"]), "b1": c(t["ffn_b1"].reshape(2, P, 1)), "wg": c(t["ffn_Wg"]),
        "bg": c(t["ffn_bg"].reshape(1, 8)), "wd": c(t["ffn_Wd"].transpose(1, 0, 2).reshape(4 * C, 8 * C)),
        "bd": c(t["ffn_bd"].reshape(1, 8 * C)), "consts": dft_constants()[0],
    }


def kernel(**inputs):
    import concourse.bacc as _bacc
    from concourse.bass_utils import run_bass_kernel_spmd as _run

    nc = _bacc.Bacc("TRN2", target_bir_lowering=False, num_devices=1)
    arrays = layout(inputs)
    args = [nc.dram_tensor(n, arrays[n].shape, F32, kind="ExternalInput").ap() for n in NAMES]
    out = nc.dram_tensor("out_0", (B, S + 1, S), F32, kind="ExternalOutput").ap()
    build(nc, *args, out, dft_constants()[1])
    r = _run(nc, [arrays], core_ids=[0])
    return r.results[0]["out_0"]
```

```python
from contextlib import ExitStack

import numpy as np

import concourse.bass as bass
from concourse import mybir

F32 = mybir.dt.float32
F32R = mybir.dt.float32r
BF16 = mybir.dt.bfloat16
ALU = mybir.AluOpType
ACT = mybir.ActivationFunctionType
AX = mybir.AxisListType

P = 128
B, C, S = 64, 64, 64
PIX = S * S
PAIRS = B // 2
KX, KY = 32, 16
LAYERS = 4
CH = 8
KC = KX // CH
MODES = KC * KY
EPS = 1e-5
T = S + 1
HEADS = 8
TT, TILES = 104, 20
HALF = TT * TILES
G_XT, G_K, G_V, G_Q, G_WO, G_WT, G_XT2, G_H, G_LG, G_Y = (
    int(n) for n in np.cumsum([0, 3, 4, 4, 32, 3, 3, 3, 10, 1]))
IMS = 7
HID = 128
SLOT = 1024
LEAD = 1
NORM = B * PIX

INV = ["mT", "ih0", "ih1", "gT0", "gT1", "iw0", "iw1", "iw2", "iw3"]
FWD = ["pw0", "pw1", "pw2", "pw3", "hT0", "hT1", "hT2", "hT3", "fw0", "fw1", "fw2", "fw3",
       "dT0", "dT1", "fh0", "fh1"]
OUT = [f"fc{k}" for k in range(8)] + ["sum"]
IN_Z = ["pw0", "pw1", "xa0", "pw2", "pw3"]
ORDER = {
    "spectrum": "hT0 hT1 hT2 hT3 fw0 fw1 fw2 fw3 dT0 dT1 fh0 fh1".split(),
    "first": "pw0 pw1 xa0 pw2 pw3".split(),
    "middle": ("hT2 hT0 mT fw2 hT1 pw2 ih0 fw1 ih1 hT3 pw3 gT1 pw0 pw1 gT0 iw2 fw3 iw3 fw0 iw0 dT1 dT0 "
               "iw1 fh1 fh0").split(),
    "last": "mT fc1 fc0 ih1 ih0 fc3 gT0 fc2 gT1 fc5 iw1 fc4 iw3 fc7 fc6 iw0 iw2 sum".split(),
}
SCALAR_ORDER = {
    "spectrum": "fw0 fw1 fw2 fw3 fh0 fh1".split(),
    "first": "pw0 pw1 xa0 pw2 pw3".split(),
    "middle": "mT fw2 fw1 ih0 ih1 gT1 pw0 gT0 fw3 pw3 pw2 fw0 iw2 iw0 pw1 iw3 iw1 fh0 fh1".split(),
    "last": "mT fc1 fc0 ih1 ih0 fc3 gT0 fc2 gT1 fc5 fc4 iw1 iw3 fc7 fc6 iw2 iw0 sum".split(),
}
VECTOR_ORDER = {
    "spectrum": "hT0 hT1 hT2 hT3 dT0 dT1".split(),
    "first": "pw0 pw1 pw2 pw3".split(),
    "middle": "hT2 hT0 mT hT1 pw2 hT3 pw3 gT1 pw0 pw1 iw2 gT0 iw3 iw0 dT1 dT0 iw1 rd0 rd2 rd3 rd1".split(),
    "last": ("mT gr1 gr0 gl1 gr3 gT0 gl3 gr2 gT1 iw1 gr5 iw3 gr4 gl5 rd3 iw0 gr7 gr6 rd1 iw2 gl7 rd2 "
               "rd0 sum").split(),
}
GPSIMD_ORDER = {
    "spectrum": "".split(),
    "first": "zs".split(),
    "middle": "lo0 lo2 zs lo3 lo1".split(),
    "last": "gl0 gl2 gl4 lo3 gl6 lo1 lo0 lo2".split(),
}


def slot_table(order):
    table = {step: n % 4 for n, step in enumerate(order)}
    if len(order) % 4 == 1:
        table[order[-1]] = 1
    return table


SLOTS = {kind: slot_table(order) for kind, order in ORDER.items()}


def quarter(step):
    return int(step[-1]) if step[-1].isdigit() else 0


def is_inverse(step):
    return step in INV or step[:2] in ("rd", "lo")


def steps_of(kind, part, order=ORDER):
    return [s for s in order[kind]
            if part == "body" or (part == "head") == is_inverse(s)]


def last_of(steps, *names):
    return max(names, key=steps.index)


def uses(kind, steps, slot):
    return sum(SLOTS[kind][s] == slot for s in steps)


def pass_uses(kind):
    return [PAIRS * uses(kind, ORDER[kind], s) for s in range(4)]


MIX_USES = [2 * CH] * 3 + [2 * CH + 1]
GROUPS, ROWS = 2, 96
FIRST_BASE = [LEAD + GROUPS * uses("spectrum", ORDER["spectrum"], s) + (s < 2) for s in range(4)]
FIRST_USES, MIDDLE_USES, LAST_USES = (pass_uses(k) for k in ("first", "middle", "last"))


def fills(kind, part, j, step, base):
    slot = SLOTS[kind][step]
    steps = steps_of(kind, part)
    n = uses(kind, steps[:steps.index(step) + 1], slot)
    if part == "head":
        return base[slot] + n
    per = uses(kind, ORDER[kind], slot)
    forward = uses(kind, steps_of(kind, "tail"), slot)
    return base[slot] + j * per + (n - forward)


def once_before(kind, j, step, base):
    slot = SLOTS[kind][step]
    order = ORDER[kind]
    n = uses(kind, order[:order.index(step) + 1], slot) - uses(kind, steps_of(kind, "tail"), slot)
    return base[slot] + (j - 1) * uses(kind, order, slot) + n




def dft_constants():
    w = np.arange(S)
    ky, kx = np.arange(KY), np.concatenate([np.arange(KX // 2), np.arange(S - KX // 2, S)])
    kw = 2 * np.pi * np.outer(ky, w) / S
    kh = 2 * np.pi * np.outer(kx, w) / S
    fw = np.zeros((2, S, P))
    for h2 in range(2):
        v = fw[h2, :, :64].reshape(S, KY, 2, 2)
        v[:, :, h2, 0] = np.cos(kw).T
        v[:, :, h2, 1] = -np.sin(kw).T
    fh = np.zeros((S, 2, 4, KX))
    fh[:, 0, 0], fh[:, 1, 0] = np.cos(kh).T, np.sin(kh).T
    fh[:, 0, 1], fh[:, 1, 1] = np.sin(kh).T, -np.cos(kh).T
    eh = np.zeros((KX, 2, 2, S, 2, 2))
    for x in range(KX):
        for y in range(2):
            eh[x, 0, y, :, y, 0], eh[x, 1, y, :, y, 0] = np.cos(kh[x]), -np.sin(kh[x])
            eh[x, 0, y, :, y, 1], eh[x, 1, y, :, y, 1] = np.sin(kh[x]), np.cos(kh[x])
    ew = np.zeros((4, KY, 2, 4, S))
    order = ky.reshape(2, KY // 2).T.reshape(-1)
    ck = (np.where(ky == 0, 1.0, 2.0)[:, None] / PIX)[order]
    for h4 in range(4):
        ew[h4, :, 0, h4], ew[h4, :, 1, h4] = ck * np.cos(kw[order]), -ck * np.sin(kw[order])
    dup = (np.arange(P)[:, None] % C == np.arange(P)[None, :] % C)
    sq = np.array([1, 2 / PIX, .5 / PIX, 2 / PIX, 1 / PIX, 1 / PIX, -1 / PIX, .5 / PIX, -.5 / PIX, 0, 0, 0]) / NORM
    av = np.array([0] * 9 + [1, .5, 0]) / NORM
    parts = [("ident", np.eye(P)), ("fw", fw.reshape(P, -1)), ("fh", fh.reshape(P, -1)),
             ("eh", eh.reshape(P, -1)), ("ew", ew.reshape(P, -1)), ("dup", dup),
             ("sq", np.tile(sq, (P, 1))), ("av", np.tile(av, (P, 1))),
             ("first", np.tile(8.0 - np.arange(8), (P, 1)))]
    where, at = {}, 0
    for name, m in parts:
        where[name] = (at, m.shape[1])
        at += m.shape[1]
    return np.concatenate([m for _, m in parts], axis=1).astype(np.float32), where


def build(nc, x_p, cls_tok, fc0_w, fc0_b, w_modes, pw_t, chan, fc1_w, fc1_b, fc2_w, fc2_b,
          wq_t, wk_t, wv_t, wo_t, w1, b1, wg, bg, wd, bd, consts, out, where):
    ctx = ExitStack()
    with ctx:
        def sb(name, shape, dt=F32):
            return ctx.enter_context(nc.sbuf_tensor(name, shape, dt))

        def sem(name):
            return ctx.enter_context(nc.semaphore(name))

        con = sb("con", [P, consts.shape[1]])

        def const(name):
            at, n = where[name]
            return con[:, at:at + n]

        ident, fw_m, fh_m, dup = (const(n) for n in ("ident", "fw", "fh", "dup"))
        inv_s = sb("inv_s", [P, 2, 512], F32R)
        inv_m = con[:, where["eh"][0]:where["eh"][0] + 512]
        eh_m, ew_m = ([inv_s[:, i, n * 256:(n + 1) * 256] for i in range(2)] for n in range(2))
        pwt = sb("pwt", [P, P])
        fc0 = sb("fc0", [P, P])
        fc1 = sb("fc1", [P, 2, HID])
        pws = sb("pws", [P, 2, P], F32R)
        fc1s = sb("fc1s", [P, 2, 2, HID], F32R)
        fc2 = sb("fc2", [P, 80], F32R)
        fc2c = sb("fc2c", [P, 1])
        fc0t = sb("fc0t", [P, P])
        w0 = sb("w0", [P, P])
        zb = sb("zb", [P, 1])
        dc = sb("dc", [P, 1])
        vec = sb("vec", [P, 3])
        chn = sb("chn", [P, LAYERS, 3])
        cur = sb("cur", [P, 3])
        zacc = sb("zacc", [P, 4])
        zsum = sb("zsum", [P, 4])
        eacc = sb("eacc", [P, 2, KY])
        esum = sb("esum", [P, 2, KY])
        zdc = sb("zdc", [P, 4])
        st = sb("st", [P, 12])
        tmp = sb("tmp", [P, 2, 12])
        mom = sb("mom", [P, 12])
        with ExitStack() as region:
            def place(name, n, dt=F32, parts=P):
                return region.enter_context(nc.sbuf_tensor(name, [parts, n], dt))[:, :]

            def place_parts(name, n):
                return place(name, 2 * n, F32R).rearrange("p (s c) -> p s c", s=2)

            zy = place("zy", PIX)
            hh = place("hh", PIX)
            hs = place_parts("hs", PIX)
            ms = place("ms", 2 * KX * KY)
            mt = place_parts("mt", 8 * P)
            gg = place("gg", KY * P)
            gt = place_parts("gt", KY * P)
            outer = region
            with ExitStack() as region:
                zo = place("zo", PIX)
                ht = place("ht", PIX)
                d1 = place("d1", KY * P)
                d1t = place("d1t", KY * P)
                d2 = place("d2", 2 * KX * KY)
                xs = place("xs", 2 * KX * KY)
                junk = place("junk", 4096, BF16)
            with ExitStack() as region:
                gf = [place(f"gf{i}", SLOT) for i in range(2)]
                g_hi = [place(f"g_hi{i}", SLOT, F32R) for i in range(8)]
                g_lo = [place(f"g_lo{i}", SLOT, F32R) for i in range(8)]
                ot = place("ot", 512, parts=16)
                ot_lo = place("ot_lo", 512, parts=16)
            region = outer
        with ExitStack() as region:
            wb = [place(f"wb{i}", 8192) for i in range(2)]
            xb = [place(f"xb{i}", 8192) for i in range(2)]
            mo = place("mo", 8192)
            mjunk2 = place("mjunk", 2048)
            mjunk = mjunk2.bitcast(BF16)
            m0 = place("m0", KX * 2 * B, parts=C)
            xp = mjunk2[0:C, 0:15 * 2 * B]

        ps = [ctx.enter_context(nc.psum_tensor(f"ps{i}", [P, SLOT], F32)) for i in range(4)]

        zd = nc.dram_tensor("z_d", [PAIRS, P, PIX], F32).ap()
        ad = nc.dram_tensor("a_d", [CH, 2, C, B, MODES], F32).ap()
        md = nc.dram_tensor("m_d", [CH, C, B, 2 * MODES], F32).ap()
        xa = nc.dram_tensor("xa_d", [GROUPS * ROWS, 2 * KX * KY], F32).ap()
        tok = nc.dram_tensor("tok_d", [B, S + 1, S], F32).ap()

        filled = [sem(f"filled{i}") for i in range(4)]
        freed = [sem(f"freed{i}") for i in range(4)]
        consts_in = sem("consts_in")
        zeroed = sem("zeroed")
        rows_zeroed = sem("rows_zeroed")
        inputs_zeroed = sem("inputs_zeroed")
        small_in = sem("small_in")
        fc2_ready = sem("fc2_ready")
        x_in = sem("x_in")
        xa_out = sem("xa_out")
        xq_in = [sem(f"xq_in{k}") for k in range(4)]
        xs_in = sem("xs_in")
        prepared = sem("prepared")
        z_in = [sem(f"z_in{k}") for k in range(4)]
        m_in = sem("m_in")
        pw_in = sem("pw_in")
        h_ready = [sem(f"h_ready{k}") for k in range(4)]
        z_out = [sem(f"z_out{k}") for k in range(4)]
        a_out = sem("a_out")
        t_out = sem("t_out")
        squared = [sem(f"squared{k}") for k in range(4)]
        z_summed = sem("z_summed")
        arena_free = sem("arena_free")
        apart = sem("apart")
        pw_split = sem("pw_split")
        fc_split = sem("fc_split")
        hi_taken = {s: sem(f"hi_taken_{s}") for s in ("mT", "gT0", "gT1")}
        h_hi = [sem(f"h_hi{k}") for k in range(4)]
        h_split = [sem(f"h_split{k}") for k in range(4)]
        g_rounded = [sem(f"g_rounded{k}") for k in range(8)]
        g_split = [sem(f"g_split{k}") for k in range(8)]
        ot_ready = sem("ot_ready")
        pw_spread = sem("pw_spread")
        w_in = [sem(f"w_in{i}") for i in range(2)]
        x1_in = [sem(f"x1_in{i}") for i in range(2)]
        x2_made = [sem(f"x2_made{i}") for i in range(2)]
        m_out = [sem(f"m_out{i}") for i in range(2)]
        m_taken = sem("m_taken")
        e_summed = sem("e_summed")
        stats = sem("stats")
        stats_chain = sem("stats_chain")
        root = sem("root")
        norm_ready = sem("norm_ready")
        cls_out = sem("cls_out")
        scale_v, shift_v = mom[:, 8:9], mom[:, 9:10]
        N_STATS = 42

        def rounds():
            def mix_base(l):
                return [FIRST_BASE[s] + FIRST_USES[s] + l * (MIX_USES[s] + MIDDLE_USES[s]) for s in range(4)]
            return mix_base

        mix_base = rounds()

        def pass_base(l):
            return [b + m for b, m in zip(mix_base(l), MIX_USES)]

        arena = sb("arena", [P, 43008])
        at = 0

        def take(n, parts=P):
            nonlocal at
            at += n
            return arena[0:parts, at - n:at]

        tokm = take(TILES * 2 * S, TT)
        xn = take(TILES * 2 * S, TT)
        xt = take(HALF)
        qt = take(HALF * HEADS)
        ct = qt
        yb = [qt[0:TT, i * 1024:(i + 1) * 1024] for i in range(2)]
        kb = take(B // 2 * 2 * T)
        vc = take(HALF)
        vv = take(B * S, T)
        k_at = at - B * S - HALF - B * T
        hid = arena[:, k_at:k_at + 4 * HALF]
        wq_m, wk_m, wv_m = take(HEADS * P), take(P), take(P)
        wo_m = take(4 * S)
        w1_m = take(2 * 2 * P)
        wg_m = take(2 * 8)
        wd_m = take(2 * 8 * C)
        bd_m = take(8 * C, TT)
        bg_m = take(8, TT)
        b1_m = take(2)
        ss = take(10 * T, TT)
        ex = take(10 * T, TT)
        qb = take(520)
        attn_t = take(1040, T)
        co = take(640, TT)
        lnw = qt[0:TT, 8192:8192 + 2560]
        red = take(40, TT)
        mean_t, var_t, rt_t, inv_t, nw_t = (take(40, TT) for _ in range(5))
        mx, sm, rc = (take(10, TT) for _ in range(3))
        lg, eq, gate = (take(320, TT) for _ in range(3))
        assert at <= 43008, at
        vd = nc.dram_tensor("v_d", [B, S * T], F32).ap()
        cd = nc.dram_tensor("c_d", [B, HEADS * T * S], F32).ap()

        weights_in = sem("weights_in")
        blank = sem("blank")
        tok_in = sem("tok_in")
        ln_root = sem("ln_root")
        link_t = sem("link_t")
        xn_ready = sem("xn_ready")
        v_out = sem("v_out")
        v_in = sem("v_in")
        qb_ready = sem("qb_ready")
        s_full, s_read = sem("s_full"), sem("s_read")
        e_ready = sem("e_ready")
        t_full, t_read = sem("t_full"), sem("t_read")
        c_full, c_read = sem("c_full"), sem("c_read")
        c_out = sem("c_out")
        c_in = sem("c_in")
        g_exp = sem("g_exp")
        res_ready = sem("res_ready")
        res_out = sem("res_out")
        tail = [b + n for b, n in zip(pass_base(LAYERS - 1), LAST_USES)]

        def gfill(g):
            return tail[g % 4] + g // 4 + 1

        block = ctx.enter_context(nc.Block())

        @block.sync
        def _(sp):
            def load_group(g):
                rows = x_p.rearrange("j r c -> (j r) c")
                sp.dma_start(hh[0:ROWS, :], rows[g * ROWS:(g + 1) * ROWS, :]).then_inc(x_in, 16)

            for s in (*filled, *freed, *z_out, *m_out, *g_split, *squared, z_summed, a_out, e_summed, t_out,
                      c_full, t_read, c_read, c_out, s_full):
                sp.sem_inc(s, LEAD)
            sp.dma_start(con[:, :], consts).then_inc(consts_in, 16)
            sp.wait_ge(rows_zeroed, 1)
            load_group(0)
            sp.wait_ge(zeroed, 1)
            for i in range(2):
                r = slice(i * C, (i + 1) * C)
                sp.dma_start(fc0[3 * i:3 * i + 3, r], fc0_w).then_inc(small_in, 16)
                sp.dma_start(fc1[r, i, :], fc1_w).then_inc(small_in, 16)
                sp.dma_start(vec[r, 0:1], fc0_b).then_inc(small_in, 16)
                sp.dma_start(chn[r, :, :], chan).then_inc(small_in, 16)
            sp.dma_start(vec[:, 1:2], fc1_b).then_inc(small_in, 16)
            sp.dma_start(vec[:, 2:3], fc2_b.to_broadcast([P, 1])).then_inc(small_in, 16)
            sp.dma_start(fc2c[:, :], fc2_w).then_inc(small_in, 16)

            def load_pw(layer):
                for i in range(2):
                    r = slice(i * C, (i + 1) * C)
                    sp.dma_start(pwt[r, r], pw_t[layer]).then_inc(pw_in, 16)

            def load_m(j):
                for i in range(2):
                    src = md[:, :, 2 * j + i, :].rearrange("c o m -> o c m")
                    dst = ms[i * C:(i + 1) * C, :].rearrange("p (c m) -> p c m", c=CH)
                    sp.dma_start(dst, src).then_inc(m_in, 16)

            def load_x(j, k):
                cols = slice(k * SLOT, (k + 1) * SLOT)
                sp.dma_start(zy[0:6, cols], x_p[j, :, cols]).then_inc(xq_in[k], 16)

            def load_xs(j):
                sp.dma_start(xs[0:6, :], xa.rearrange("(j r) m -> j r m", r=6)[j]).then_inc(xs_in, 16)

            def run_pass(kind, q, base):
                def iteration(part, j, more=True):
                    order = steps_of(kind, part)
                    for step in order:
                        done = (kind, part, j, step, base)
                        slot = SLOTS[kind][step]
                        if step.startswith("pw"):
                            k = int(step[2])
                            sp.wait_ge(freed[slot], fills(*done))
                            sp.sem_inc(apart, 1)
                            sp.dma_start(zd[j - 1, :, k * SLOT:(k + 1) * SLOT],
                                         zo[:, k * SLOT:(k + 1) * SLOT]).then_inc(z_out[k], 16)
                            if kind == "first" and more:
                                load_x(j, k)
                        if step.startswith("xa") and more:
                            sp.wait_ge(filled[slot], fills(*done))
                            load_xs(j)
                        if step == "mT" and more:
                            sp.wait_ge(filled[slot], fills(*done))
                            load_m(j + 1)
                        if step.startswith("iw") and more:
                            k = quarter(step)
                            sp.wait_ge(h_ready[k], (q - 1) * PAIRS + j + 1)
                            sp.sem_inc(apart, 1)
                            sp.dma_start(zy[:, k * SLOT:(k + 1) * SLOT],
                                         zd[j + 1, :, k * SLOT:(k + 1) * SLOT]).then_inc(z_in[k], 16)
                        if kind == "spectrum" and step == "hT3" and j < GROUPS:
                            for k in range(4):
                                sp.wait_ge(filled[SLOTS[kind][f"hT{k}"]], fills(kind, part, j, f"hT{k}", base))
                            load_group(j)
                        names = ("xa0",) if kind == "first" else ("fh0", "fh1")
                        if step in names and step == last_of(order, *names):
                            for name in names:
                                sp.wait_ge(freed[SLOTS[kind][name]], fills(kind, part, j, name, base))
                                sp.sem_inc(apart, 1)
                            if kind == "spectrum":
                                sp.dma_start(xa[(j - 1) * ROWS:j * ROWS, :], d2[0:ROWS, :]).then_inc(xa_out, 16)
                                continue
                            for i in range(2):
                                for b in range(2):
                                    src = d2[i * C:(i + 1) * C, b * 512:(b + 1) * 512]
                                    dst = ad[:, b, :, 2 * (j - 1) + i, :].rearrange("k c m -> c k m")
                                    sp.dma_start(dst, src.rearrange("p (k m) -> p k m", k=CH))\
                                        .then_inc(a_out, 16)
                        if step == "sum":
                            sp.wait_ge(freed[slot], fills(*done))
                            dst = tok[bass.ds(2 * (j - 1), 2), 1:S + 1, :] if not isinstance(j, int) else \
                                tok[2 * (j - 1):2 * j, 1:S + 1, :]
                            for i in range(2):
                                sp.dma_start(dst[i].rearrange("(t r) w -> t (r w)", t=8),
                                             ot[8 * i:8 * i + 8, :]).then_inc(t_out, 16)

                if kind == "spectrum":
                    for g in range(GROUPS):
                        iteration("tail", g + 1)
                    return
                if kind == "first":
                    sp.wait_ge(inputs_zeroed, 1)
                    for k in range(4):
                        load_x(0, k)
                    sp.wait_ge(xa_out, 16 * GROUPS)
                    load_xs(0)
                    with sp.Fori(1, PAIRS) as j:
                        iteration("body", j)
                    iteration("tail", PAIRS, more=False)
                    return
                load_m(0)
                for k in range(4):
                    sp.dma_start(zy[:, k * SLOT:(k + 1) * SLOT],
                                 zd[0, :, k * SLOT:(k + 1) * SLOT]).then_inc(z_in[k], 16)
                iteration("head", 0)
                with sp.Fori(1, PAIRS - 1) as j:
                    iteration("body", j)
                iteration("body", PAIRS - 1, more=False)
                iteration("tail", PAIRS)

            def value(n):
                return n if isinstance(n, int) else sp.snap(sp.to_reg(n))

            def run_mix(l):
                base = mix_base(l)

                def load(c, par):
                    for row in range(2):
                        sp.dma_start(xb[par][row * C:(row + 1) * C, 0:4096],
                                     ad[c, row].rearrange("c b m -> c (b m)")).then_inc(x1_in[par], 16)
                    sp.dma_start(wb[par][:, 0:4096], w_modes[l, c]).then_inc(w_in[par], 16)

                def store(c, par):
                    sp.wait_ge(freed[3], base[3] + 2 * (c + 1))
                    sp.dma_start(md[c].rearrange("o b m -> o (b m)"),
                                 mo[par * C:(par + 1) * C, :]).then_inc(m_out[par], 16)

                z_count, a_count, pairs, m_count = (
                    value(LEAD + n * (l + 1)) for n in (16 * PAIRS, 4 * 16 * PAIRS, PAIRS, 16 * (CH // 2)))
                for k in range(4):
                    sp.wait_ge(z_out[k], z_count)
                sp.wait_ge(a_out, a_count)
                for k in range(4):
                    sp.wait_ge(squared[k], pairs)
                sp.wait_ge(z_summed, pairs)
                sp.sem_inc(arena_free, 1)
                load(0, 0)
                load(1, 1)
                with sp.Fori(0, CH // 2 - 1) as i:
                    for par in range(2):
                        sp.wait_ge(filled[3], base[3] + 2 * (2 * i + par + 1))
                        sp.sem_inc(apart, 1)
                        load(2 * i + par + 2, par)
                        store(2 * i + par, par)
                for par in range(2):
                    store(CH - 2 + par, par)
                for par in range(2):
                    sp.wait_ge(m_out[par], m_count)

            load_pw(0)
            run_pass("spectrum", 0, [LEAD] * 4)
            run_pass("first", 0, FIRST_BASE)
            with sp.Fori(0, LAYERS - 1) as l:
                run_mix(l)
                load_pw(l + 1)
                run_pass("middle", l + 1, pass_base(l))
            run_mix(LAYERS - 1)
            run_pass("last", LAYERS, pass_base(LAYERS - 1))
            sp.wait_ge(t_out, LEAD + 32 * PAIRS)

            sp.dma_start(tok[:, 0, :], cls_tok.to_broadcast([B, S])).then_inc(cls_out, 16)
            sp.wait_ge(cls_out, 16)

            def tokens(a):
                return [a[i * 32:(i + 1) * 32].rearrange("b t c -> (b t) c").rearrange("(n p) c -> p n c", p=TT)
                        for i in range(2)]

            tv = tokm.rearrange("p (n i c) -> p i n c", i=2, c=S)
            for i in range(2):
                sp.dma_start(tv[:, i], tokens(tok)[i]).then_inc(tok_in, 16)
            sp.wait_ge(blank, 1)
            for i in range(2):
                r = slice(i * C, (i + 1) * C)
                dst = wq_m[r].rearrange("p (h e) -> p h e", h=HEADS)[:, :, r]
                sp.dma_start(dst, wq_t.rearrange("c (h d) -> c h d", h=HEADS)).then_inc(weights_in, 16)
                sp.dma_start(wk_m[r, r], wk_t).then_inc(weights_in, 16)
                sp.dma_start(wv_m[r, r], wv_t).then_inc(weights_in, 16)
                sp.dma_start(w1_m[r, i * 2 * P:(i + 1) * 2 * P], w1).then_inc(weights_in, 16)
                sp.dma_start(wg_m[:, 8 * i:8 * i + 8], wg[i * P:(i + 1) * P, :]).then_inc(weights_in, 16)
                sp.dma_start(wd_m[:, i * 512:(i + 1) * 512], wd[i * P:(i + 1) * P, :]).then_inc(weights_in, 16)
                sp.dma_start(b1_m[:, i:i + 1], b1[i]).then_inc(weights_in, 16)
            sp.dma_start(wo_m.rearrange("p (k o) -> p k o", k=4),
                         wo_t.rearrange("(k p) o -> p k o", p=P)).then_inc(weights_in, 16)
            sp.dma_start(bd_m, bd.to_broadcast([TT, 8 * C])).then_inc(weights_in, 16)
            sp.dma_start(bg_m, bg.to_broadcast([TT, 8])).then_inc(weights_in, 16)
            sp.wait_ge(freed[(G_V + 3) % 4], gfill(G_V + 3))
            for i in range(2):
                sp.dma_start(vd[i * 32:(i + 1) * 32].rearrange("b (o t) -> o b t", t=T),
                             vc[i * C:(i + 1) * C].rearrange("p (b t) -> p b t", t=T)).then_inc(v_out, 16)
            sp.wait_ge(v_out, 32)
            sp.dma_start(vv.rearrange("p (b d) -> p b d", d=S),
                         vd.rearrange("b (t d) -> t b d", d=S)).then_inc(v_in, 16)

            def store_context(b):
                sp.wait_ge(c_read, LEAD + b + 1)
                for i in range(2):
                    src = co[:, i * 320:(i + 1) * 320].rearrange("p (n d) -> p n d", d=S)
                    sp.dma_start(cd[b + 32 * i].rearrange("(n p d) -> p n d", p=TT, d=S), src).then_inc(c_out, 16)

            def load_context(b):
                sp.wait_ge(c_out, LEAD + 32 * (b + 1))
                sp.sem_inc(apart, 1)
                for i in range(2):
                    src = cd[b + 32 * i].rearrange("(k p t) -> p k t", k=4, t=T)
                    dst = ct[:, bass.ds(b * 520 + i * 260, 260)].rearrange("p (k t) -> p k t", t=T)
                    sp.dma_start(dst, src).then_inc(c_in, 16)

            store_context(0)
            with sp.Fori(1, 32) as b:
                store_context(b)
                load_context(b - 1)
            load_context(31)
            sp.wait_ge(res_ready, 1)
            for i in range(2):
                sp.dma_start(tokens(out)[i], tv[:, i]).then_inc(res_out, 16)
            sp.wait_ge(res_out, 32)

        @block.tensor
        def _(pe):
            def turn(out_, in_):
                n = in_.shape[0]
                return pe.transpose(out_, in_, ident[0:n, 0:n])

            def three(out_, stationary, moving):
                pe.matmul(out_, stationary[0], moving[0], start=True, stop=False)
                pe.matmul(out_, stationary[0], moving[1], start=False, stop=False)
                return pe.matmul(out_, stationary[1], moving[0], start=False, stop=True)

            def parts(a, at, n):
                return [a[:, i, at:at + n] for i in range(2)]

            def run_pass(kind, q, base):
                def emptied(step, part, j):
                    pe.wait_ge(freed[SLOTS[kind][step]], fills(kind, part, j, step, base))

                def all_emptied(steps, part, j):
                    for slot in range(4):
                        here = [s for s in steps if SLOTS[kind][s] == slot]
                        if here:
                            emptied(last_of(ORDER[kind], *here), part, j)

                def iteration(part, j):
                    for step in steps_of(kind, part):
                        slot = SLOTS[kind][step]
                        n = fills(kind, part, j, step, base)
                        o = ps[slot]
                        pe.wait_ge(freed[slot], n - 1)
                        if step == "mT":
                            pe.wait_ge(m_in, 2 * 16 * ((q - 1) * PAIRS + j + 1))
                            v = ms.rearrange("p (k y) -> p k y", y=8)
                            for i in range(8):
                                mm = turn(o[:, i * P:(i + 1) * P], v[:, :, i])
                        elif step in ("ih0", "ih1"):
                            a = int(step[2])
                            emptied("mT", part, j)
                            for i in range(4):
                                mm = three(o[:, i * 256:(i + 1) * 256], parts(mt, (4 * a + i) * P, P), eh_m)
                        elif step in ("gT0", "gT1"):
                            a = int(step[2])
                            all_emptied(["ih0", "ih1"], part, j)
                            for i in range(8):
                                mm = turn(o[:, i * P:(i + 1) * P], gg[:, (8 * a + i) * P:(8 * a + i + 1) * P])
                        elif step.startswith("pw") and kind == "first":
                            k = int(step[2])
                            pe.wait_ge(xq_in[k], 16 * j)
                            for i in range(2):
                                mm = pe.matmul(o[:, i * 512:(i + 1) * 512], w0[:, :],
                                               zy[:, (2 * k + i) * 512:(2 * k + i + 1) * 512],
                                               start=True, stop=True)
                        elif step.startswith("xa"):
                            pe.wait_ge(xs_in, 16 * j)
                            for i in range(2):
                                mm = pe.matmul(o[:, i * 512:(i + 1) * 512], fc0[:, :],
                                               xs[:, i * 512:(i + 1) * 512], start=True, stop=True)
                        elif step.startswith("iw"):
                            k = int(step[2])
                            emptied(f"gT{k // 2}", part, j)
                            for i in range(4):
                                mm = three(o[:, i * 256:(i + 1) * 256], parts(gt, (4 * k + i) * P, P), ew_m)
                        elif step.startswith("pw"):
                            k = int(step[2])
                            pe.wait_ge(h_split[k], (q - 1) * PAIRS + j)
                            for i in range(2):
                                mm = three(o[:, i * 512:(i + 1) * 512], parts(pws, 0, P),
                                           parts(hs, (2 * k + i) * 512, 512))
                        elif step.startswith("hT"):
                            k = int(step[2])
                            if kind == "spectrum":
                                pe.wait_ge(x_in, 16 * j)
                            else:
                                pe.wait_ge(h_ready[k], (q - 1) * PAIRS + j)
                            for i in range(8):
                                mm = turn(o[:, i * P:(i + 1) * P], hh[:, (8 * k + i) * P:(8 * k + i + 1) * P])
                        elif step in ("fw0", "fw1", "fw2", "fw3"):
                            k = int(step[2])
                            emptied(f"hT{k}", part, j)
                            for i in range(8):
                                mm = pe.matmul(o[:, i * P:i * P + 96],
                                               ht[:, (8 * k + i) * P:(8 * k + i + 1) * P], fw_m[:, 0:96],
                                               start=True, stop=True)
                        elif step in ("dT0", "dT1"):
                            a = int(step[2])
                            all_emptied([f"fw{k}" for k in range(4)], part, j)
                            for i in range(8):
                                mm = turn(o[:, i * P:(i + 1) * P], d1[:, (8 * a + i) * P:(8 * a + i + 1) * P])
                        elif step in ("fh0", "fh1"):
                            a = int(step[2])
                            emptied(f"dT{a}", part, j)
                            for i in range(8):
                                mm = pe.matmul(o[:, i * P:i * P + 96],
                                               d1t[:, (8 * a + i) * P:(8 * a + i + 1) * P], fh_m[:, 0:96],
                                               start=True, stop=True)
                        elif step.startswith("fc"):
                            i, k = divmod(int(step[2]), 4)
                            pe.wait_ge(h_split[k], (q - 1) * PAIRS + j)
                            for n2 in range(2):
                                mm = three(o[:, n2 * 512:(n2 + 1) * 512], [fc1s[:, s, i, :] for s in range(2)],
                                           parts(hs, (2 * k + n2) * 512, 512))
                        elif step == "sum":
                            for r in range(16):
                                k, c = divmod(r, 2)
                                if c == 0:
                                    pe.wait_ge(g_split[k], LEAD + j)
                                for g in (g_hi, g_lo):
                                    mm = pe.matmul(o[0:64, 0:512], fc2[:, 15 - r:79 - r], g[k][:, c * 512:(c + 1) * 512],
                                                   start=(r == 0 and g is g_hi), stop=(r == 15 and g is g_lo))
                        mm.then_inc(filled[slot], 1)

                if kind == "spectrum":
                    for g in range(GROUPS):
                        iteration("tail", g + 1)
                    return
                if kind == "first":
                    pe.wait_ge(freed[0], base[0] - 1)
                    turn(ps[0][:, 0:P], fc0[:, :]).then_inc(filled[0], 1)
                    pe.wait_ge(prepared, 1)
                    pe.wait_ge(pw_in, 2 * 16)
                    pe.wait_ge(freed[1], base[1] - 1)
                    pe.matmul(ps[1][:, 0:P], fc0t[:, :], pwt[:, :], start=True, stop=True)
                    pe.matmul(ps[1][:, 512:513], pwt[:, :], vec[:, 0:1], start=True, stop=True)\
                        .then_inc(filled[1], 1)
                    pe.wait_ge(prepared, 4)
                if kind == "middle":
                    pe.wait_ge(pw_split, 2 * q)
                iteration("head", 0)
                with pe.Fori(1, PAIRS) as j:
                    iteration("body", j)
                iteration("tail", PAIRS)

            def run_mix(l):
                base = mix_base(l)
                with pe.Fori(0, CH // 2) as i:
                    for par in range(2):
                        pe.wait_ge(pw_spread, 2 * l + par + 1)
                        pe.wait_ge(x2_made[par], l * (CH // 2) + i + 1)
                        pe.wait_ge(w_in[par], 16 * (l * (CH // 2) + i + 1))
                        w = wb[par].rearrange("p (o m) -> p o m", m=MODES)
                        v = xb[par].rearrange("p (h b m) -> p h b m", h=2, m=MODES)
                        for g in range(8):
                            slot = g % 4
                            pe.wait_ge(freed[slot], base[slot] + 4 * i + 2 * par + g // 4)
                            for n in range(8):
                                y, kx = divmod(n, KC)
                                m = kx * KY + 2 * g + y
                                mm = pe.matmul(ps[slot][:, n * P:(n + 1) * P], w[:, :, m], v[:, :, :, m],
                                               start=True, stop=True)
                            mm.then_inc(filled[slot], 1)
                pe.wait_ge(stats, l + 1)
                pe.wait_ge(freed[3], base[3] + 2 * CH)
                pe.matmul(ps[3][:, 0:12], dup, st[:, :], start=True, stop=True).then_inc(filled[3], 1)

            pe.wait_ge(consts_in, 16)
            pe.wait_ge(small_in, 16 * 11)
            pe.wait_ge(fc2_ready, 2)
            run_pass("spectrum", 0, [LEAD] * 4)
            run_pass("first", 0, FIRST_BASE)
            with pe.Fori(0, LAYERS - 1) as l:
                run_mix(l)
                run_pass("middle", l + 1, pass_base(l))
            run_mix(LAYERS - 1)
            pe.wait_ge(fc2_ready, 3)
            pe.wait_ge(fc_split, 3)
            run_pass("last", LAYERS, pass_base(LAYERS - 1))

            def fill(g):
                pe.wait_ge(freed[g % 4], gfill(g) - 1)
                return ps[g % 4]

            def transposes(first, ready):
                pe.wait_ge(xn_ready, ready)
                for g in range(3):
                    o = fill(first + g)
                    for i in range(8 * g, min(8 * g + 8, TILES)):
                        at = (i % 8) // 4 * 512 + i % 4 * TT
                        mm = turn(o[:, at:at + TT], xn[:, i * P:(i + 1) * P])
                    mm.then_inc(filled[(first + g) % 4], 1)

            def project(first, weights):
                for n in range(4):
                    o = fill(first + n)
                    for i in range(2):
                        mm = pe.matmul(o[:, i * 512:i * 512 + 260], weights,
                                       xt[:, (2 * n + i) * 260:(2 * n + i + 1) * 260], start=True, stop=True)
                    mm.then_inc(filled[(first + n) % 4], 1)

            transposes(G_XT, 1)
            pe.wait_ge(weights_in, 17 * 16)
            pe.wait_ge(freed[(G_XT + 2) % 4], gfill(G_XT + 2))
            project(G_K, wk_m)
            project(G_V, wv_m)
            for h in range(HEADS):
                project(G_Q + 4 * h, wq_m[:, h * P:(h + 1) * P])

            def scores(b):
                pe.wait_ge(qb_ready, b + 1)
                if not (isinstance(b, int) and b == 0):
                    pe.wait_ge(s_read, b)
                for i in range(5):
                    at = i // 3 * 512 + i % 3 * 130
                    mm = pe.matmul(ps[0][0:TT, at:at + 130], qb[:, i * TT:(i + 1) * TT],
                                   kb[:, bass.ds(b * 130, 130)], start=True, stop=True)
                mm.then_inc(s_full, 1)

            def turned(b):
                pe.wait_ge(e_ready, b + 1)
                pe.wait_ge(t_read, LEAD + b)
                for i in range(5):
                    for half in range(2):
                        n = half * 5 + i
                        o = ps[1 + n // 8][0:T, n % 8 // 4 * 512 + n % 4 * TT:n % 8 // 4 * 512 + (n % 4 + 1) * TT]
                        mm = turn(o, ex[:, (2 * i + half) * T:(2 * i + half + 1) * T])
                mm.then_inc(t_full, 1)

            def context(b):
                pe.wait_ge(t_read, LEAD + b + 1)
                pe.wait_ge(c_read, LEAD + b)
                for half in range(2):
                    for i in range(5):
                        mm = pe.matmul(ps[3][0:TT, half * 512 + i * S:half * 512 + (i + 1) * S],
                                       attn_t[:, (half * 5 + i) * TT:(half * 5 + i + 1) * TT],
                                       vv[:, bass.ds((half * 32 + b) * S, S)], start=True, stop=True)
                mm.then_inc(c_full, 1)

            for g in range(G_WO - 4, G_WO):
                pe.wait_ge(freed[g % 4], gfill(g))
            pe.wait_ge(v_in, 16)
            scores(0)
            with pe.Fori(1, 32) as b:
                turned(b - 1)
                scores(b)
                context(b - 1)
            turned(31)
            context(31)

            pe.wait_ge(c_in, 64 * 16)
            pe.wait_ge(c_read, LEAD + 32)
            cv = ct.rearrange("p (b x) -> p b x", b=32)
            for g in range(3):
                o = fill(G_WO + g)
                for u in range(2 * g, min(2 * g + 2, 5)):
                    first, end = u * IMS, min((u + 1) * IMS, 32)
                    for half in range(2):
                        for k in range(4):
                            at = (half * 4 + k) * T
                            mm = pe.matmul(o[half * C:(half + 1) * C, u % 2 * 512:u % 2 * 512 + (end - first) * T],
                                           wo_m[:, k * S:(k + 1) * S], cv[:, first:end, at:at + T],
                                           start=(k == 0), stop=(k == 3))
                mm.then_inc(filled[(G_WO + g) % 4], 1)
            pe.wait_ge(freed[(G_WO + 2) % 4], gfill(G_WO + 2))
            for g in range(3):
                o = fill(G_WT + g)
                for i in range(8 * g, min(8 * g + 8, TILES)):
                    mm = turn(o[0:TT, i % 8 * P:(i % 8 + 1) * P], xt[:, i * TT:(i + 1) * TT])
                mm.then_inc(filled[(G_WT + g) % 4], 1)
            transposes(G_XT2, 2)
            pe.wait_ge(freed[(G_XT2 + 2) % 4], gfill(G_XT2 + 2))
            for g in range(10):
                o = fill(G_H + g)
                for u in range(2 * g, 2 * g + 2):
                    hc, rest = divmod(u, 10)
                    half, n = divmod(rest, 5)
                    w = w1_m[:, half * 2 * P + hc * P:half * 2 * P + (hc + 1) * P]
                    mm = pe.matmul(o[:, u % 2 * 512:u % 2 * 512 + 416], w, xt[:, n * 416:(n + 1) * 416],
                                   start=True, stop=True)
                mm.then_inc(filled[(G_H + g) % 4], 1)

            def hidden(n, hc):
                i, half = divmod(n, 2)
                at = (hc * 2 + half) * HALF + i * TT
                return hid[:, at:at + TT]

            o = fill(G_LG)
            pe.wait_ge(freed[(G_H + 9) % 4], gfill(G_H + 9))
            for n in range(40):
                for hc in range(2):
                    mm = pe.matmul(o[0:TT, n * 8:n * 8 + 8], hidden(n, hc), wg_m[:, hc * 8:hc * 8 + 8],
                                   start=(hc == 0), stop=(hc == 1))
            mm.then_inc(filled[G_LG % 4], 1)
            for g in range(20):
                o = fill(G_Y + g)
                for i in range(2):
                    for hc in range(2):
                        mm = pe.matmul(o[0:TT, i * 512:(i + 1) * 512], hidden(2 * g + i, hc),
                                       wd_m[:, hc * 512:(hc + 1) * 512], start=(hc == 0), stop=(hc == 1))
                mm.then_inc(filled[(G_Y + g) % 4], 1)

        @block.vector
        def _(dve):
            def run_pass(kind, q, base):
                def iteration(part, j):
                    for step in steps_of(kind, part, VECTOR_ORDER):
                        k = quarter(step)
                        cols = slice(k * SLOT, (k + 1) * SLOT)
                        if step in SLOTS[kind]:
                            slot = SLOTS[kind][step]
                            n = fills(kind, part, j, step, base)
                            o = ps[slot]
                        if step.startswith("hT"):
                            dve.wait_ge(filled[slot], n)
                            dve.tensor_copy(ht[:, cols], o[:, :]).then_inc(freed[slot], 1)
                        elif step.startswith("dT"):
                            dve.wait_ge(filled[slot], n)
                            dve.tensor_copy(d1t[:, cols], o[:, :]).then_inc(freed[slot], 1)
                        elif step == "mT" or step.startswith("gT"):
                            dst = mt if step == "mT" else gt[:, :, cols]
                            dve.wait_ge(hi_taken[step], (q - 1) * PAIRS + j + 1)
                            dve.tensor_tensor(dst[:, 1], o[:, :], dst[:, 0], ALU.subtract).then_inc(freed[slot], 1)
                        elif step.startswith("iw"):
                            dve.wait_ge(z_in[k], 16 * ((q - 1) * PAIRS + j + 1))
                            dve.wait_ge(filled[slot], n)
                            dve.tensor_tensor(zy[:, cols], o[:, :], zy[:, cols], ALU.add)\
                                .then_inc(freed[slot], 1)
                        elif step.startswith("pw"):
                            dve.wait_ge(z_out[k], LEAD + 16 * (q * PAIRS + j - 1))
                            dve.wait_ge(squared[k], LEAD + q * PAIRS + j - 1)
                            dve.wait_ge(filled[slot], n)
                            if kind == "first":
                                dve.tensor_scalar(zo[:, cols], o[:, :], zb[:, :], None, ALU.add)\
                                    .then_inc(freed[slot], 1)
                            else:
                                dve.tensor_copy(zo[:, cols], o[:, :]).then_inc(freed[slot], 1)
                        elif step == "sum":
                            dve.wait_ge(t_out, LEAD + 32 * (j - 1))
                            dve.wait_ge(ot_ready, j)
                            dve.tensor_tensor(ot, o[0:16, 0:512], ot_lo, ALU.add).then_inc(freed[slot], 1)
                        elif step.startswith("rd"):
                            reader = f"fc{4 + k}" if kind == "last" else f"pw{k}"
                            dve.wait_ge(h_ready[k], (q - 1) * PAIRS + j + 1)
                            if part == "body":
                                dve.wait_ge(filled[SLOTS[kind][reader]], fills(kind, part, j, reader, base))
                            dve.tensor_copy(hs[:, 0, cols], hh[:, cols]).then_inc(h_hi[k], 1)
                        elif step.startswith("gr"):
                            fc = f"fc{k}"
                            dve.wait_ge(freed[SLOTS[kind][fc]], fills(kind, part, j, fc, base))
                            dve.wait_ge(filled[SLOTS[kind]["sum"]], once_before(kind, j, "sum", base))
                            dve.tensor_copy(g_hi[k], gf[k % 2]).then_inc(g_rounded[k], 1)
                        elif step.startswith("gl"):
                            dve.wait_ge(g_rounded[k], j)
                            dve.tensor_tensor(g_lo[k], gf[k % 2], g_hi[k], ALU.subtract).then_inc(g_split[k], 1)

                if kind == "spectrum":
                    for g in range(GROUPS):
                        iteration("tail", g + 1)
                    return
                if kind == "first":
                    dve.wait_ge(filled[0], base[0])
                    dve.tensor_copy(fc0t[:, :], ps[0][:, 0:P]).then_inc(prepared, 1)
                    dve.wait_ge(prepared, 1)
                    dve.tensor_scalar(dc[:, :], vec[:, 0:1], float(PIX), None, ALU.mult).then_inc(prepared, 1)
                    dve.wait_ge(filled[1], base[1])
                    dve.tensor_copy(w0[:, :], ps[1][:, 0:P]).then_inc(prepared, 1)
                    dve.tensor_copy(zb[:, :], ps[1][:, 512:513]).then_inc(prepared, 1)
                    dve.wait_ge(prepared, 4)
                    for k in range(2):
                        dve.sem_inc(freed[k], 1)
                if kind == "middle":
                    dve.wait_ge(pw_in, 2 * 16 * (q + 1))
                    dve.tensor_copy(pws[:, 0], pwt[:, :]).then_inc(pw_split, 1)
                    dve.wait_ge(pw_split, 2 * q - 1)
                    dve.tensor_tensor(pws[:, 1], pwt[:, :], pws[:, 0], ALU.subtract).then_inc(pw_split, 1)
                iteration("head", 0)
                with dve.Fori(1, PAIRS) as j:
                    iteration("body", j)
                iteration("tail", PAIRS)

            def run_mix(l):
                base = mix_base(l)
                dve.wait_ge(arena_free, l + 1)
                dve.wait_ge(pw_in, 2 * 16 * (l + 1))
                def spread(par):
                    w = wb[par][:, 4096:8192].rearrange("p (o m) -> p o m", m=MODES)
                    dve.memset(w[C:P], 0.0)
                    dve.tensor_scalar(w[0:C], pwt[0:C, 0:C].unsqueeze(2).to_broadcast([C, C, MODES]),
                                      2.0, None, ALU.mult).then_inc(pw_spread, 1)

                def swap(i, par, part):
                    x = xb[par]
                    half, cols = part // 2, slice(part % 2 * 2048, part % 2 * 2048 + 2048)
                    if part == 0:
                        dve.wait_ge(x1_in[par], 2 * 16 * (l * (CH // 2) + i + 1))
                    if half == 0:
                        last = dve.tensor_scalar(x[0:C, 4096:8192][:, cols], x[C:P, cols], -1.0, None, ALU.mult)
                    else:
                        last = dve.tensor_copy(x[C:P, 4096:8192][:, cols], x[0:C, cols])
                    if part == 3:
                        last.then_inc(x2_made[par], 1)

                def chunk_pair(i, end):
                    for par in range(2):
                        more = not (end and par == 1)
                        m = mo[par * C:(par + 1) * C, :].rearrange("p (b k y) -> p b y k", b=B, y=KY)
                        for g in range(8):
                            slot = g % 4
                            dve.wait_ge(m_taken, 8 * ((l * (CH // 2) + i) * 2 + par) + g + 1)
                            if par == 0 and g == 0:
                                dve.tensor_reduce(zdc[C:P, bass.ds(i, 1)], ps[slot][C:P, 0:B], AX.X, ALU.add)
                            for y in range(2):
                                col = slice(slot * SLOT + y * 512, slot * SLOT + (y + 1) * 512)
                                z = ps[slot][C:P, y * 512:(y + 1) * 512].rearrange("p (k b) -> p b k", b=B)
                                last = dve.tensor_tensor_reduce(
                                    mjunk[C:P, col].rearrange("p (b k) -> p b k", b=B), z, m[:, :, 2 * g + y],
                                    1.0, 0.0, ALU.mult, ALU.add, eacc[C:P, par, 2 * g + y:2 * g + y + 1])
                            last.then_inc(freed[slot], 1)
                            if more and 1 <= g < 5:
                                swap(i + par, 1 - par, g - 1)

                spread(0)
                for part in range(4):
                    swap(0, 0, part)
                spread(1)
                with dve.Fori(0, CH // 2 - 1) as i:
                    chunk_pair(i, False)
                chunk_pair(CH // 2 - 1, True)

                chain = [l * N_STATS]

                def link(ins):
                    chain[0] = chain[0] + 1
                    ins.then_inc(stats_chain, 1)
                    dve.wait_ge(stats_chain, chain[0])

                start = chain[0]
                dve.wait_ge(e_summed, LEAD + (CH // 2) * (l + 1))
                dve.wait_ge(z_summed, LEAD + PAIRS * (l + 1))
                link(dve.memset(st[:, :], 0.0))
                link(dve.tensor_reduce(st[:, 0:1], zsum[:, :], AX.X, ALU.add))
                link(dve.tensor_reduce(st[0:C, 1:2], esum[0:C, :, 1:KY], AX.XY, ALU.add))
                link(dve.tensor_reduce(st[0:C, 2:3], esum[0:C, :, 0], AX.X, ALU.add))
                link(dve.tensor_reduce(st[C:P, 3:4], esum[C:P, :, 1:KY], AX.XY, ALU.add))
                link(dve.tensor_reduce(st[C:P, 4:5], esum[C:P, :, 0], AX.X, ALU.add))
                for k in range(1, KX // 2):
                    link(dve.tensor_tensor(xp[:, (k - 1) * P:k * P], m0[:, k * P:(k + 1) * P],
                                           m0[:, (KX - k) * P:(KX - k + 1) * P], ALU.mult))
                v = xp.rearrange("p (k r b) -> p r k b", r=2, b=B)
                link(dve.tensor_reduce(st[0:C, 5:6], v[:, 0], AX.XY, ALU.add))
                link(dve.tensor_reduce(st[0:C, 6:7], v[:, 1], AX.XY, ALU.add))
                link(dve.tensor_tensor(xp[:, 0:P], m0[:, 0:P], m0[:, 0:P], ALU.mult))
                link(dve.tensor_reduce(st[0:C, 7:8], xp[:, 0:B], AX.X, ALU.add))
                link(dve.tensor_reduce(st[0:C, 8:9], xp[:, B:P], AX.X, ALU.add))
                link(dve.tensor_reduce(st[0:C, 9:10], m0[:, 0:B], AX.X, ALU.add))
                link(dve.tensor_copy(st[C:P, 10:11], zdc[C:P, 0:1]))
                dve.memset(zsum[:, :], 0.0)
                dve.memset(esum[:, :, :], 0.0)
                dve.memset(tmp[:, 0, 0:1], 0.0).then_inc(stats, 1)
                dve.wait_ge(filled[3], base[3] + 2 * CH + 1)
                link(dve.tensor_tensor(tmp[:, 0, :], ps[3][:, 0:12], const("sq"), ALU.mult))
                dve.tensor_tensor(tmp[:, 1, :], ps[3][:, 0:12], const("av"), ALU.mult).then_inc(freed[3], 1)
                dve.wait_ge(freed[3], base[3] + 2 * CH + 1)
                link(dve.tensor_reduce(mom[:, 0:2], tmp[:, :, :], AX.X, ALU.add))
                sq, mean = mom[:, 0:1], mom[:, 1:2]
                link(dve.tensor_tensor(mom[:, 2:3], mean, mean, ALU.mult))
                link(dve.tensor_tensor(mom[:, 3:4], sq, mom[:, 2:3], ALU.subtract))
                dve.tensor_scalar(mom[:, 4:5], mom[:, 3:4], 0.0, EPS, ALU.max, ALU.add).then_inc(root, 1)
                dve.wait_ge(root, 2 * (l + 1))
                link(dve.reciprocal(mom[:, 6:7], mom[:, 5:6]))
                link(dve.tensor_tensor(mom[:, 7:8], mom[:, 6:7], mom[:, 6:7], ALU.mult))
                link(dve.tensor_tensor(mom[:, 7:8], mom[:, 7:8], mom[:, 4:5], ALU.mult))
                link(dve.tensor_scalar(mom[:, 7:8], mom[:, 7:8], -0.5, 1.5, ALU.mult, ALU.add))
                link(dve.tensor_tensor(mom[:, 6:7], mom[:, 7:8], mom[:, 6:7], ALU.mult))
                layer = chn[:, bass.ds(l, 1), :] if not isinstance(l, int) else chn[:, l:l + 1, :]
                link(dve.tensor_copy(cur[:, :].unsqueeze(1), layer))
                gamma, beta, pwb = (cur[:, i:i + 1] for i in range(3))
                link(dve.tensor_tensor(scale_v, gamma, mom[:, 6:7], ALU.mult))
                link(dve.tensor_tensor(mom[:, 10:11], mean, pwb, ALU.add))
                link(dve.tensor_tensor(mom[:, 10:11], pwb, mom[:, 10:11], ALU.subtract))
                link(dve.tensor_tensor(mom[:, 10:11], mom[:, 10:11], scale_v, ALU.mult))
                dve.tensor_tensor(shift_v, mom[:, 10:11], beta, ALU.add).then_inc(norm_ready, 1)
                n = chain[0] - start
                assert not isinstance(l, int) or n == N_STATS, n

            dve.memset(hh, 0.0).then_inc(rows_zeroed, 1)
            dve.memset(pwt[:, :], 0.0)
            dve.memset(fc0[:, :], 0.0)
            dve.memset(fc1[:, :, :], 0.0)
            dve.memset(fc2[:, :].bitcast(F32), 0.0)
            dve.memset(zdc[:, :], 0.0)
            dve.memset(zsum[:, :], 0.0)
            dve.memset(esum[:, :, :], 0.0)
            dve.memset(eacc[:, :, :], 0.0).then_inc(zeroed, 1)
            dve.wait_ge(zeroed, 1)
            dve.wait_ge(small_in, 16 * 11)
            dve.wait_ge(consts_in, 16)
            dve.tensor_copy(inv_s[:, 0], inv_m).then_inc(fc2_ready, 1)
            dve.wait_ge(fc2_ready, 1)
            dve.tensor_tensor(inv_s[:, 1], inv_m, inv_s[:, 0], ALU.subtract).then_inc(fc2_ready, 1)
            dve.tensor_copy(fc2[:, 15:16], fc2c[:, :]).then_inc(fc_split, 1)
            dve.wait_ge(fc_split, 1)
            dve.tensor_tensor(fc2[:, 47:48], fc2c[:, :], fc2[:, 15:16], ALU.subtract).then_inc(fc_split, 1)
            dve.wait_ge(fc_split, 2)
            dve.tensor_copy(fc1s[:, 0], fc1[:, :, :]).then_inc(fc2_ready, 1)
            dve.wait_ge(fc2_ready, 3)
            dve.tensor_tensor(fc1s[:, 1], fc1[:, :, :], fc1s[:, 0], ALU.subtract).then_inc(fc_split, 1)
            run_pass("spectrum", 0, [LEAD] * 4)
            run_pass("first", 0, FIRST_BASE)
            with dve.Fori(0, LAYERS - 1) as l:
                run_mix(l)
                run_pass("middle", l + 1, pass_base(l))
            run_mix(LAYERS - 1)
            run_pass("last", LAYERS, pass_base(LAYERS - 1))

            links = [0]

            def link(ins):
                links[0] = links[0] + 1
                ins.then_inc(link_t, 1)
                dve.wait_ge(link_t, links[0])

            dve.wait_ge(t_out, LEAD + 32 * PAIRS)
            for m in (kb, wq_m, wk_m, wv_m):
                dve.memset(m, 0.0)
            dve.memset(w1_m, 0.0).then_inc(blank, 1)

            def rows(a):
                return a.rearrange("p (n c) -> p n c", c=S)

            def wide(a, n=S):
                return a.unsqueeze(2).to_broadcast([TT, a.shape[1], n])

            def norm(turn):
                link(dve.tensor_reduce(red, rows(tokm), AX.X, ALU.add))
                link(dve.tensor_scalar(mean_t, red, 1.0 / S, None, ALU.mult))
                link(dve.tensor_tensor(rows(xn), rows(tokm), wide(mean_t), ALU.subtract))
                link(dve.tensor_tensor(lnw, xn, xn, ALU.mult))
                link(dve.tensor_reduce(red, rows(lnw), AX.X, ALU.add))
                dve.tensor_scalar(var_t, red, 1.0 / S, EPS, ALU.mult, ALU.add).then_inc(ln_root, 1)
                dve.wait_ge(ln_root, 2 * turn)
                link(dve.reciprocal(inv_t, rt_t))
                link(dve.tensor_tensor(nw_t, inv_t, inv_t, ALU.mult))
                link(dve.tensor_tensor(nw_t, nw_t, var_t, ALU.mult))
                link(dve.tensor_scalar(nw_t, nw_t, -0.5, 1.5, ALU.mult, ALU.add))
                link(dve.tensor_tensor(inv_t, inv_t, nw_t, ALU.mult))
                dve.tensor_tensor(rows(xn), rows(xn), wide(inv_t), ALU.mult).then_inc(xn_ready, 1)

            def transposed(first):
                for g in range(3):
                    dve.wait_ge(filled[(first + g) % 4], gfill(first + g))
                    n = 2 if g < 2 else 1
                    src = ps[(first + g) % 4][:, 0:n * 512].rearrange("p (k c) -> p k c", k=n)[:, :, 0:416]
                    dve.tensor_copy(xt[:, g * 832:g * 832 + n * 416].rearrange("p (k c) -> p k c", k=n), src)\
                        .then_inc(freed[(first + g) % 4], 1)

            def pair(g, n=260):
                return ps[g % 4][:, :].rearrange("p (k c) -> p k c", k=2)[:, :, 0:n]

            dve.wait_ge(tok_in, 32)
            norm(1)
            transposed(G_XT)
            for g in range(G_V, G_V + 4):
                dve.wait_ge(filled[g % 4], gfill(g))
                n = g - G_V
                dve.tensor_copy(vc[:, n * 520:(n + 1) * 520].rearrange("p (k c) -> p k c", k=2), pair(g))\
                    .then_inc(freed[g % 4], 1)
            for g in range(G_Q + 1, G_Q + 32, 2):
                dve.wait_ge(filled[g % 4], gfill(g))
                h, n = divmod(g - G_Q, 4)
                dst = qt.rearrange("p (t h) -> p t h", h=HEADS)[:, n * 520:(n + 1) * 520, h]
                dve.tensor_copy(dst.rearrange("p (k c) -> p k c", k=2), pair(g)).then_inc(freed[g % 4], 1)

            start = links[0]
            N_LOOP = 3

            def softmax(b):
                dve.wait_ge(s_full, LEAD + b + 1)
                for a, e in ((0, 3), (3, 5)):
                    v = ps[0][0:TT, a // 3 * 512:a // 3 * 512 + (e - a) * 130].rearrange("p (n t) -> p n t", t=T)
                    last = dve.tensor_reduce(mx[:, 2 * a:2 * e], v, AX.X, ALU.max)
                link(last)
                for a, e in ((0, 3), (3, 5)):
                    v = ps[0][0:TT, a // 3 * 512:a // 3 * 512 + (e - a) * 130].rearrange("p (n t) -> p n t", t=T)
                    d = ss[:, 2 * a * T:2 * e * T].rearrange("p (n t) -> p n t", t=T)
                    last = dve.tensor_tensor(d, v, wide(mx[:, 2 * a:2 * e], T), ALU.subtract)
                last.then_inc(s_read, 1)

            def sums(b):
                dve.wait_ge(e_ready, b + 1)
                link(dve.tensor_reduce(sm, ex.rearrange("p (n t) -> p n t", t=T), AX.X, ALU.add))
                link(dve.reciprocal(rc, sm))

            def normalise(b):
                dve.wait_ge(c_full, LEAD + b + 1)
                dve.wait_ge(c_out, LEAD + 32 * b)
                for half in range(2):
                    src = ps[3][0:TT, half * 512:half * 512 + 320].rearrange("p (n d) -> p n d", d=S)
                    dst = co[:, half * 320:(half + 1) * 320].rearrange("p (n d) -> p n d", d=S)
                    r = rc.rearrange("p (n h) -> p h n", h=2)[:, half]
                    last = dve.tensor_tensor(dst, src, wide(r), ALU.mult)
                last.then_inc(c_read, 1)

            softmax(0)
            sums(0)
            after_first = links[0]
            with dve.Fori(1, 32) as b:
                links[0] = (b - 1) * N_LOOP + after_first
                softmax(b)
                normalise(b - 1)
                dve.wait_ge(c_read, LEAD + b)
                sums(b)
            links[0] = after_first + 31 * N_LOOP
            normalise(31)

            for g in range(3):
                dve.wait_ge(filled[(G_WO + g) % 4], gfill(G_WO + g))
                for u in range(2 * g, min(2 * g + 2, 5)):
                    a, e = u * IMS * T, min((u + 1) * IMS * T, HALF)
                    last = dve.tensor_copy(xt[:, a:e], ps[(G_WO + g) % 4][:, u % 2 * 512:u % 2 * 512 + e - a])
                last.then_inc(freed[(G_WO + g) % 4], 1)
            for g in range(3):
                dve.wait_ge(filled[(G_WT + g) % 4], gfill(G_WT + g))
                a, e = g * SLOT, min((g + 1) * SLOT, 2560)
                dve.tensor_tensor(tokm[:, a:e], ps[(G_WT + g) % 4][0:TT, 0:e - a], tokm[:, a:e], ALU.add)\
                    .then_inc(freed[(G_WT + g) % 4], 1)
            dve.wait_ge(freed[(G_WT + 2) % 4], gfill(G_WT + 2))
            norm(2)
            transposed(G_XT2)

            def by_token(a):
                return a.rearrange("p (n e) -> p n e", e=8)

            dve.wait_ge(filled[G_LG % 4], gfill(G_LG))
            dve.tensor_tensor(by_token(lg), by_token(ps[G_LG % 4][0:TT, 0:320]),
                              bg_m.unsqueeze(1).to_broadcast([TT, 40, 8]), ALU.add).then_inc(freed[G_LG % 4], 1)
            dve.wait_ge(freed[G_LG % 4], gfill(G_LG))
            link(dve.tensor_reduce(red, by_token(lg), AX.X, ALU.max))
            dve.tensor_tensor(by_token(lg), by_token(lg), wide(red, 8), ALU.subtract).then_inc(g_exp, 1)
            dve.wait_ge(g_exp, 2)
            link(dve.tensor_reduce(red, by_token(gate), AX.X, ALU.add))
            link(dve.reciprocal(inv_t, red))
            link(dve.tensor_reduce(red, by_token(gate), AX.X, ALU.max))
            link(dve.tensor_tensor(by_token(eq), by_token(gate), wide(red, 8), ALU.is_equal))
            link(dve.tensor_tensor(by_token(eq), by_token(eq),
                                   const("first")[0:TT].unsqueeze(1).to_broadcast([TT, 40, 8]), ALU.mult))
            link(dve.tensor_reduce(red, by_token(eq), AX.X, ALU.max))
            link(dve.tensor_tensor(by_token(eq), by_token(eq), wide(red, 8), ALU.is_equal))
            link(dve.tensor_tensor(by_token(gate), by_token(gate), wide(inv_t, 8), ALU.mult))
            link(dve.tensor_tensor(gate, gate, eq, ALU.mult))
            for g in range(20):
                y = yb[g % 2]
                yv = y.rearrange("p (n e c) -> p n e c", n=2, c=C)
                dve.wait_ge(filled[(G_Y + g) % 4], gfill(G_Y + g))
                for i in range(2):
                    last = dve.tensor_tensor(y[:, i * 512:(i + 1) * 512], ps[(G_Y + g) % 4][0:TT, i * 512:(i + 1) * 512],
                                             bd_m, ALU.add)
                last.then_inc(freed[(G_Y + g) % 4], 1)
                dve.wait_ge(freed[(G_Y + g) % 4], gfill(G_Y + g))
                for i in range(2):
                    gt_i = by_token(gate)[:, 2 * g + i]
                    last = dve.tensor_tensor(yv[:, i], yv[:, i], wide(gt_i, C), ALU.mult)
                link(last)
                link(dve.tensor_reduce(rows(xn)[:, 2 * g:2 * g + 2], yv.rearrange("p n e c -> p n c e"),
                                       AX.X, ALU.add))
            dve.tensor_tensor(tokm, tokm, xn, ALU.add).then_inc(res_ready, 1)

        @block.scalar
        def _(act):
            def run_pass(kind, q, base):
                def iteration(part, j):
                    for step in steps_of(kind, part, SCALAR_ORDER):
                        k = quarter(step)
                        cols = slice(k * SLOT, (k + 1) * SLOT)
                        slot = SLOTS[kind][step]
                        n = fills(kind, part, j, step, base)
                        o = ps[slot]
                        if step in ("fw0", "fw1", "fw2", "fw3"):
                            act.wait_ge(filled[slot], n)
                            dst = d1.rearrange("p (y t x) -> p t y x", y=KY, x=4)[:, 8 * k:8 * k + 8]
                            src = o[:, :].rearrange("p (t c) -> p t c", t=8)[:, :, 0:64]
                            act.copy(dst, src.rearrange("p t (y x) -> p t y x", x=4)).then_inc(freed[slot], 1)
                        elif step in ("fh0", "fh1"):
                            if kind == "spectrum":
                                act.wait_ge(xa_out, 16 * (j - 1))
                            else:
                                act.wait_ge(a_out, LEAD + 4 * 16 * (q * PAIRS + j - 1))
                            act.wait_ge(filled[slot], n)
                            dst = d2.rearrange("p (m y) -> p y m", y=KY)[:, 8 * k:8 * k + 8]
                            src = o[:, :].rearrange("p (y m) -> p y m", y=8)[:, :, 0:64]
                            act.copy(dst, src).then_inc(freed[slot], 1)
                        elif step == "mT":
                            act.wait_ge(filled[slot], n)
                            act.copy(mt[:, 0], o[:, :]).then_inc(hi_taken[step], 1)
                        elif step.startswith("gT"):
                            act.wait_ge(filled[slot], n)
                            act.copy(gt[:, 0, cols], o[:, :]).then_inc(hi_taken[step], 1)
                        elif step.startswith("ih"):
                            act.wait_ge(filled[slot], n)
                            dst = gg.rearrange("p (h y x) -> p y h x", y=8, x=4)[:, 4 * k:4 * k + 4]
                            act.copy(dst, o[:, :].rearrange("p (y h x) -> p y h x", y=4, x=4))\
                                .then_inc(freed[slot], 1)
                        elif step.startswith("iw"):
                            act.wait_ge(freed[slot], n)
                            if part == "head":
                                act.wait_ge(norm_ready, q)
                            act.activation(hh[:, cols], zy[:, cols], ACT.Gelu, bias=shift_v,
                                           scale=scale_v).then_inc(h_ready[k], 1)
                        elif step.startswith("pw"):
                            act.wait_ge(freed[slot], n)
                            act.wait_ge(z_summed, LEAD + q * PAIRS + j - 1)
                            act.activation(junk[:, cols], zo[:, cols], ACT.Square,
                                           accum_out=zacc[:, k:k + 1]).then_inc(squared[k], 1)
                        elif step.startswith("xa"):
                            act.wait_ge(a_out, LEAD + 4 * 16 * (j - 1))
                            act.wait_ge(filled[slot], n)
                            act.activation(d2[:, 0:1], o[:, 0:1], ACT.Identity, bias=dc[:, :])
                            act.copy(d2[:, 1:], o[:, 1:]).then_inc(freed[slot], 1)
                        elif step.startswith("fc"):
                            e = int(step[2])
                            act.wait_ge(g_split[(e - 2) % 8], LEAD + j - (e < 2))
                            act.wait_ge(filled[slot], n)
                            act.activation(gf[e % 2], o[:, :], ACT.Gelu, bias=vec[:, 1:2]).then_inc(freed[slot], 1)
                        elif step == "sum":
                            act.wait_ge(freed[slot], once_before(kind, j, "sum", base))
                            act.wait_ge(filled[slot], n)
                            act.activation(ot_lo, o[32:48, 0:512], ACT.Identity, bias=vec[32:48, 2:3])\
                                .then_inc(ot_ready, 1)

                if kind == "spectrum":
                    for g in range(GROUPS):
                        iteration("tail", g + 1)
                    return
                if kind == "first":
                    act.wait_ge(prepared, 4)
                iteration("head", 0)
                with act.Fori(1, PAIRS) as j:
                    iteration("body", j)
                iteration("tail", PAIRS)

            def run_mix(l):
                base = mix_base(l)
                act.wait_ge(arena_free, l + 1)
                with act.Fori(0, CH // 2) as i:
                    act.wait_ge(e_summed, LEAD + l * (CH // 2) + i)
                    for par in range(2):
                        act.wait_ge(m_out[par], LEAD + 16 * (l * (CH // 2) + i))
                        for g in range(8):
                            slot = g % 4
                            act.wait_ge(filled[slot], base[slot] + 4 * i + 2 * par + g // 4 + 1)
                            src = ps[slot][0:C, :].rearrange("p (y k b) -> p b y k", b=B, y=2)
                            dst = mo[par * C:(par + 1) * C, :].rearrange("p (b k y) -> p b y k", b=B, y=KY)
                            act.copy(dst[:, :, 2 * g:2 * g + 2], src)
                            if g == 0:
                                act.copy(m0[:, bass.ds((2 * i + par) * 512, 512)], ps[slot][0:C, 0:512])
                            for a, e, col in ([(0, 8, 0), (8, 16, 1)] if g == 0 else [(0, 16, 2 * g)]):
                                last = act.activation(mjunk[0:C, slot * SLOT + a * B:slot * SLOT + e * B],
                                                      ps[slot][0:C, a * B:e * B], ACT.Square,
                                                      accum_out=eacc[0:C, par, col:col + 1])
                            last.then_inc(m_taken, 1)
                act.wait_ge(root, 2 * l + 1)
                act.activation(mom[:, 5:6], mom[:, 4:5], ACT.Sqrt).then_inc(root, 1)

            act.wait_ge(small_in, 16 * 11)
            run_pass("spectrum", 0, [LEAD] * 4)
            run_pass("first", 0, FIRST_BASE)
            with act.Fori(0, LAYERS - 1) as l:
                run_mix(l)
                run_pass("middle", l + 1, pass_base(l))
            run_mix(LAYERS - 1)
            run_pass("last", LAYERS, pass_base(LAYERS - 1))

            act.wait_ge(ln_root, 1)
            act.activation(rt_t, var_t, ACT.Sqrt).then_inc(ln_root, 1)
            act.wait_ge(blank, 1)

            def pair(g, n=260):
                return ps[g % 4][:, :].rearrange("p (k c) -> p k c", k=2)[:, :, 0:n]

            for g in range(G_K, G_K + 4):
                act.wait_ge(filled[g % 4], gfill(g))
                n = g - G_K
                for half in range(2):
                    r = slice(half * C, (half + 1) * C)
                    dst = kb[r].rearrange("p (b h t) -> p h b t", h=2, t=T)[:, half, 8 * n:8 * n + 8]
                    for k in range(2):
                        last = act.copy(dst[:, 4 * k:4 * k + 4],
                                        pair(g)[r, k].rearrange("p (b t) -> p b t", t=T))
                last.then_inc(freed[g % 4], 1)
            for g in range(G_Q, G_Q + 32, 2):
                act.wait_ge(filled[g % 4], gfill(g))
                h, n = divmod(g - G_Q, 4)
                dst = qt.rearrange("p (t h) -> p t h", h=HEADS)[:, n * 520:(n + 1) * 520, h]
                act.copy(dst.rearrange("p (k c) -> p k c", k=2), pair(g)).then_inc(freed[g % 4], 1)

            def exponentials(b):
                act.wait_ge(s_read, b + 1)
                act.activation(ex, ss, ACT.Exp, scale=1.0 / np.sqrt(8.0)).then_inc(e_ready, 1)

            def turned(b):
                act.wait_ge(t_full, b + 1)
                act.wait_ge(c_full, LEAD + b)
                act.copy(attn_t[:, 0:832].rearrange("p (k c) -> p k c", k=2),
                         ps[1][0:T, :].rearrange("p (k c) -> p k c", k=2)[:, :, 0:416])
                act.copy(attn_t[:, 832:1040], ps[2][0:T, 0:208]).then_inc(t_read, 1)

            exponentials(0)
            with act.Fori(1, 32) as b:
                turned(b - 1)
                exponentials(b)
            turned(31)
            act.wait_ge(ln_root, 3)
            act.activation(rt_t, var_t, ACT.Sqrt).then_inc(ln_root, 1)
            for g in range(G_H, G_H + 10):
                act.wait_ge(filled[g % 4], gfill(g))
                n, hc = g - G_H, (g - G_H) // 5
                act.activation(hid[:, n * 832:(n + 1) * 832].rearrange("p (k c) -> p k c", k=2), pair(g, 416),
                               ACT.Gelu, bias=b1_m[:, hc:hc + 1]).then_inc(freed[g % 4], 1)
            act.wait_ge(g_exp, 1)
            act.activation(gate, lg, ACT.Exp).then_inc(g_exp, 1)

        @block.gpsimd
        def _(pool):
            def run_pass(kind, q, base):
                def iteration(part, j):
                    for step in steps_of(kind, part, GPSIMD_ORDER):
                        k = quarter(step)
                        cols = slice(k * SLOT, (k + 1) * SLOT)
                        if step.startswith("lo"):
                            pool.wait_ge(h_hi[k], (q - 1) * PAIRS + j + 1)
                            pool.tensor_tensor(hs[:, 1, cols], hh[:, cols], hs[:, 0, cols], ALU.subtract)\
                                .then_inc(h_split[k], 1)
                        elif step.startswith("gl"):
                            pool.wait_ge(g_rounded[k], j)
                            pool.tensor_tensor(g_lo[k], gf[k % 2], g_hi[k], ALU.subtract).then_inc(g_split[k], 1)
                        elif step == "zs":
                            for i in range(4):
                                pool.wait_ge(squared[i], LEAD + q * PAIRS + j)
                            pool.wait_ge(z_summed, LEAD + q * PAIRS + j - 1)
                            pool.tensor_tensor(zsum[:, :], zsum[:, :], zacc[:, :], ALU.add).then_inc(z_summed, 1)

                if kind == "spectrum":
                    return
                pool.wait_ge(zeroed, 1)
                if not (isinstance(q, int) and q == 0):
                    pool.wait_ge(norm_ready, q)
                iteration("head", 0)
                with pool.Fori(1, PAIRS) as j:
                    iteration("body", j)
                iteration("tail", PAIRS)

            def run_mix(l):
                base = mix_base(l)
                with pool.Fori(0, CH // 2) as i:
                    pool.wait_ge(freed[3], base[3] + 4 * (i + 1))
                    pool.wait_ge(e_summed, LEAD + l * (CH // 2) + i)
                    pool.tensor_tensor(esum[:, :, :], esum[:, :, :], eacc[:, :, :], ALU.add)\
                        .then_inc(e_summed, 1)

            pool.memset(xs, 0.0)
            pool.memset(zy, 0.0).then_inc(inputs_zeroed, 1)
            run_pass("spectrum", 0, [LEAD] * 4)
            run_pass("first", 0, FIRST_BASE)
            with pool.Fori(0, LAYERS - 1) as l:
                run_mix(l)
                run_pass("middle", l + 1, pass_base(l))
            run_mix(LAYERS - 1)
            run_pass("last", LAYERS, pass_base(LAYERS - 1))

            for g in range(G_WO - 4, G_WO):
                pool.wait_ge(freed[g % 4], gfill(g))
            with pool.Fori(0, 32) as b:
                pool.wait_ge(s_full, LEAD + b)
                pool.tensor_copy(qb, qt[:, bass.ds(b * 520, 520)]).then_inc(qb_ready, 1)


NAMES = ["x_p", "cls_tok", "fc0_w", "fc0_b", "w_modes", "pw_t", "chan", "fc1_w", "fc1_b", "fc2_w", "fc2_b",
         "wq_t", "wk_t", "wv_t", "wo_t", "w1", "b1", "wg", "bg", "wd", "bd", "consts"]


def layout(t):
    def c(a):
        return np.ascontiguousarray(a)

    t = {k.replace("L0_", ""): np.asarray(v) for k, v in t.items()}
    x = t["x"].reshape(PAIRS, 2, PIX, 3).transpose(0, 1, 3, 2).reshape(PAIRS, 6, PIX)
    w = np.stack([np.stack([t["tok_w1r"], t["tok_w2r"]]), np.stack([t["tok_w1i"], t["tok_w2i"]])])
    w = w.reshape(2, 2, LAYERS, C, C, CH // 2, MODES)
    w = w.transpose(2, 1, 5, 0, 3, 4, 6).reshape(LAYERS, CH, P, C * MODES)
    chan = np.stack([t["tok_gamma"], t["tok_beta"], t["tok_pw_b"]], axis=-1).transpose(1, 0, 2)
    return {
        "x_p": c(x), "cls_tok": c(t["cls_tok"].reshape(1, S)), "fc0_w": c(t["tok_fc0_w"]),
        "fc0_b": c(t["tok_fc0_b"].reshape(C, 1)), "w_modes": c(w), "pw_t": c(t["tok_pw_w"].transpose(0, 2, 1)),
        "chan": c(chan), "fc1_w": c(t["tok_fc1_w"]), "fc1_b": c(t["tok_fc1_b"].reshape(HID, 1)),
        "fc2_w": c(t["tok_fc2_w"]), "fc2_b": c(t["tok_fc2_b"].reshape(1, 1)),
        "wq_t": c(t["attn_Wq"].T), "wk_t": c(t["attn_Wk"].T), "wv_t": c(t["attn_Wv"].T), "wo_t": c(t["attn_Wo"].T),
        "w1": c(t["ffn_W1"]), "b1": c(t["ffn_b1"].reshape(2, P, 1)), "wg": c(t["ffn_Wg"]),
        "bg": c(t["ffn_bg"].reshape(1, 8)), "wd": c(t["ffn_Wd"].transpose(1, 0, 2).reshape(4 * C, 8 * C)),
        "bd": c(t["ffn_bd"].reshape(1, 8 * C)), "consts": dft_constants()[0],
    }


def kernel(**inputs):
    import concourse.bacc as _bacc
    from concourse.bass_utils import run_bass_kernel_spmd as _run

    nc = _bacc.Bacc("TRN2", target_bir_lowering=False, num_devices=1)
    arrays = layout(inputs)
    args = [nc.dram_tensor(n, arrays[n].shape, F32, kind="ExternalInput").ap() for n in NAMES]
    out = nc.dram_tensor("out_0", (B, S + 1, S), F32, kind="ExternalOutput").ap()
    build(nc, *args, out, dft_constants()[1])
    r = _run(nc, [arrays], core_ids=[0])
    return r.results[0]["out_0"]
```
